# Optimizing a Trainium2 kernel written in Bass

```python
import numpy as np
import jax
import jax.numpy as jnp

def _softmax(x, axis=-1):
    return jax.nn.softmax(x, axis=axis)

def _gelu(x):
    return jax.nn.gelu(x, approximate=True)

def _silu(x):
    return jax.nn.silu(x)

def _sigmoid(x):
    return jax.nn.sigmoid(x)

def _layernorm(x, axis=-1, eps=1e-05):
    m = jnp.mean(x, axis=axis, keepdims=True)
    v = jnp.var(x, axis=axis, keepdims=True)
    return (x - m) / jnp.sqrt(v + eps)

def _scatter_add(tgt, idx, src, axis=0):
    return tgt.at[idx].add(src)

def _segment_sum(src, seg, n):
    return jax.ops.segment_sum(src, seg, n)
kernel_name = 'mk_gnn_ffn_d1_gnn_r8_7d8d88'

def setup_inputs(seed: int=0):
    np.random.seed(seed)
    _w = jnp.asarray

    def _rec_inputs():
        import jax
        import jax.numpy as jnp
        _gk = jax.random.key(seed)
        x = -0.0002117 + 1 * jax.random.normal(jax.random.fold_in(_gk, 1), (1250, 512), jnp.float32)
        src = jax.random.randint(jax.random.fold_in(_gk, 2), (40000,), 0, 1250, jnp.int32)
        dst = jnp.minimum((1250 * jax.random.uniform(jax.random.fold_in(_gk, 3), (40000,)) ** 2.0).astype(jnp.int32), 9999)
        _o = jnp.argsort(dst, stable=True)
        src = src[_o]
        dst = dst[_o]
        return (x, src, dst)
    x, src, dst = _rec_inputs()

    def _L0_gnn_setup():
        import jax, jax.numpy as jnp
        import numpy as np
        N_NODES = 6250
        N_EDGES = 100000
        D_IN = 512
        D_HID = 16

        def _gcn_conv(x, src, dst, W, b):
            n = x.shape[0]
            ones = jnp.ones(src.shape, dtype=x.dtype)
            deg = jax.ops.segment_sum(ones, dst, num_segments=n)
            dinv = jnp.where(deg > 0, jax.lax.rsqrt(deg), 0.0)
            norm = dinv[src] * dinv[dst]
            h = x @ W
            msg = h[src] * norm[:, None]
            return jax.ops.segment_sum(msg, dst, num_segments=n) + b
        key = jax.random.key(seed)
        k1, k2, k3, k4, k5 = jax.random.split(key, 5)
        x = jax.random.normal(k1, (N_NODES, D_IN), dtype=jnp.float32)
        src = jax.random.randint(k2, (N_EDGES,), 0, N_NODES, dtype=jnp.int64)
        dst = jax.random.randint(k3, (N_EDGES,), 0, N_NODES, dtype=jnp.int64)
        edge_index = jnp.stack([src, dst], axis=0)
        W1 = jax.random.normal(k4, (D_IN, D_HID), dtype=jnp.float32) * (1.0 / np.sqrt(D_IN))
        b1 = jnp.zeros((D_HID,), dtype=jnp.float32)
        W2 = jax.random.normal(k5, (D_HID, D_IN), dtype=jnp.float32) * (1.0 / np.sqrt(D_HID))
        b2 = jnpep = jnp.zeros((D_IN,), dtype=jnp.float32)
        return {'x': x, 'edge_index': edge_index, 'W1': W1, 'b1': b1, 'W2': W2, 'b2': b2}
    _L0_gnn_all = _L0_gnn_setup()
    _L0_gnn_in = {k: v for k, v in _L0_gnn_all.items() if k in ('W1', 'b1', 'W2', 'b2')}
    del _L0_gnn_all

    def _L0_ffn_setup():
        import jax, jax.numpy as jnp
        import numpy as np
        B, S, D = (8, 512, 512)
        H = 256
        O = 512
        E = 8
        TOP_K = 1
        key = jax.random.key(seed)
        ks = jax.random.split(key, 8)
        sc = 0.02
        return {'x': jax.random.normal(ks[0], (B, S, D), dtype=jnp.float32), 'Wr': jax.random.normal(ks[1], (D, E), dtype=jnp.float32) * sc, 'br': jnp.zeros((E,), dtype=jnp.float32), 'W1': jax.random.normal(ks[2], (E, D, H), dtype=jnp.float32) * sc, 'b1': jnp.zeros((E, H), dtype=jnp.float32), 'W2': jax.random.normal(ks[3], (E, H, O), dtype=jnp.float32) * sc, 'b2': jnp.zeros((E, O), dtype=jnp.float32)}
    _L0_ffn_all = _L0_ffn_setup()
    _L0_ffn_in = {k: v for k, v in _L0_ffn_all.items() if k in ('Wr', 'br', 'W1', 'b1', 'W2', 'b2')}
    del _L0_ffn_all
    return {'x': x, 'src': src, 'dst': dst, 'L0_gnn_W1': _L0_gnn_in['W1'], 'L0_gnn_b1': _L0_gnn_in['b1'], 'L0_gnn_W2': _L0_gnn_in['W2'], 'L0_gnn_b2': _L0_gnn_in['b2'], 'L0_ffn_Wr': _L0_ffn_in['Wr'], 'L0_ffn_br': _L0_ffn_in['br'], 'L0_ffn_W1': _L0_ffn_in['W1'], 'L0_ffn_b1': _L0_ffn_in['b1'], 'L0_ffn_W2': _L0_ffn_in['W2'], 'L0_ffn_b2': _L0_ffn_in['b2']}

def reference(x, src, dst, L0_gnn_W1, L0_gnn_b1, L0_gnn_W2, L0_gnn_b2, L0_ffn_Wr, L0_ffn_br, L0_ffn_W1, L0_ffn_b1, L0_ffn_W2, L0_ffn_b2):
    import jax
    import jax.numpy as jnp

    def _L0_gnn_ref(x, edge_index, W1, b1, W2, b2):
        import jax, jax.numpy as jnp
        import numpy as np
        N_NODES = 6250
        N_EDGES = 100000
        D_IN = 512
        D_HID = 16

        def _gcn_conv(x, src, dst, W, b):
            n = x.shape[0]
            ones = jnp.ones(src.shape, dtype=x.dtype)
            deg = jax.ops.segment_sum(ones, dst, num_segments=n)
            dinv = jnp.where(deg > 0, jax.lax.rsqrt(deg), 0.0)
            norm = dinv[src] * dinv[dst]
            h = x @ W
            msg = h[src] * norm[:, None]
            return jax.ops.segment_sum(msg, dst, num_segments=n) + b
        n = x.shape[0]
        loop = jnp.arange(n, dtype=edge_index.dtype)
        src = jnp.concatenate([edge_index[0], loop])
        dst = jnp.concatenate([edge_index[1], loop])
        h = _gcn_conv(x, src, dst, W1, b1)
        h = jax.nn.relu(h)
        out = _gcn_conv(h, src, dst, W2, b2)
        return out

    def _L0_ffn_ref(x, Wr, br, W1, b1, W2, b2):
        import jax, jax.numpy as jnp
        import numpy as np
        B, S, D = (8, 512, 512)
        H = 256
        O = 512
        E = 8
        TOP_K = 1
        b, s, d = x.shape
        xf = x.reshape(-1, d)
        router_logits = xf @ Wr + br
        topk_logits, topk_idx = jax.lax.top_k(router_logits, TOP_K)
        topk_gates = jax.nn.softmax(topk_logits, axis=1)
        out = jnp.zeros((xf.shape[0], O), dtype=x.dtype)
        for k in range(TOP_K):
            idx_k = topk_idx[:, k]
            gate_k = topk_gates[:, k:k + 1]
            for e in range(E):
                h = jax.nn.relu(xf @ W1[e] + b1[e])
                oe = h @ W2[e] + b2[e]
                mask = (idx_k == e)[:, None]
                out = out + jnp.where(mask, gate_k * oe, 0.0)
        return out.reshape(b, s, O)
    edge_index = jnp.stack([src, dst])
    x = x + _L0_gnn_ref(_layernorm(x, axis=-1), edge_index, L0_gnn_W1, L0_gnn_b1, L0_gnn_W2, L0_gnn_b2)
    x = x + _L0_ffn_ref(_layernorm(x, axis=-1)[None], L0_ffn_Wr, L0_ffn_br, L0_ffn_W1, L0_ffn_b1, L0_ffn_W2, L0_ffn_b2)[0]
    return x

_drawn_inputs = setup_inputs


def setup_inputs(seed=0):
    import zlib

    import numpy as np

    out = dict(_drawn_inputs(seed))
    spreads = {'L0_gnn_b1': (0.0, 0.1),
     'L0_gnn_b2': (0.0, 0.1),
     'L0_ffn_br': (0.0, 0.1),
     'L0_ffn_b1': (0.0, 0.375),
     'L0_ffn_b2': (0.0, 0.1)}
    factors = {}
    for name, (base, spread) in spreads.items():
        noise = np.random.default_rng([zlib.crc32(name.encode()), seed]).standard_normal(out[name].shape)
        drawn = base * np.exp(spread * noise) if base else spread * noise
        out[name] = jnp.asarray(drawn.astype(out[name].dtype))
    for name, factor in factors.items():
        out[name] = (out[name] * factor).astype(out[name].dtype)
    return out
```

```python
import concourse.bass as bass
from concourse import mybir
from contextlib import ExitStack

F32 = mybir.dt.float32
BF16 = mybir.dt.bfloat16
I16 = mybir.dt.int16
I32 = mybir.dt.int32
ALU = mybir.AluOpType
ACT = mybir.ActivationFunctionType
X = mybir.AxisListType.X

N = 1250
D = 512
P = 128
NT = 10
TAIL = N - (NT - 1) * P
NB, EL, KE = 160, 250, 125
NC = 2 * NB
WD = 20
MC = NT * WD
GB, NG = 4, NB // 4
RING = 3
PR = 5
WS = 40
NWS, MS = NT * P // WS, NT * WS
NE, HID = 8, 256
SLOTS = (N - NE) // P + NE
ROW = D + 4
NOBODY = 1 << 20
EPS = 1e-5
GH = 16
G48 = 3 * GH


def program(nc, x, edges, dst, gW1, gb1, gW2, gb2, Wr, br, fW1, fb1, fW2, fb2, out):
    ctx = ExitStack()
    with ctx:
        def sb(name, shape, dt):
            return ctx.enter_context(nc.sbuf_tensor(name, shape, dt))

        def sem(name):
            return ctx.enter_context(nc.semaphore(name))

        routed = nc.dram_tensor("routed", [SLOTS * P, ROW], F32, kind="Internal").ap()

        xt = sb("xt", [P, NT, ROW], F32)
        w1 = sb("w1", [P, NE, 4, HID], F32)
        w2 = sb("w2", [P, NE, 2, D], F32)
        b1t = sb("b1t", [P, 2, NE], F32)
        b2f = sb("b2f", [P, NE, D], F32)
        ct = [sb(f"ct{i}", [P, NT, NT * P], BF16) for i in range(2)]
        oh = sb("oh", [KE, RING, GB, P, 2], BF16)
        mvr = sb("mv", [P, RING * GB * MC * 2], BF16)
        mv = mvr[0:KE, :].rearrange("p (n g k c) -> p n g k c", n=RING, g=GB, k=MC)
        ir2 = sb("ir2", [KE, P, 2], I16)
        im2 = sb("im2", [KE, MC, 2], I16)
        R16 = sb("R16", [KE, NC], I16)
        Q16 = sb("Q16", [KE, NC], I16)
        G16 = sb("G16", [KE, NC], I16)
        D16 = sb("D16", [KE, NC], I16)
        row = sb("row", [1, 2, NB], F32)
        wl = sb("wl", [1, 8], F32)
        baseI = sb("baseI", [1, NB], I32)
        badI = sb("badI", [1, 2], I32)
        vio = sb("vio", [P, NT + 1], F32)
        onesf = sb("onesf", [P, P], F32)
        identf = sb("identf", [P, P], F32)
        identb = sb("identb", [P, P], BF16)
        upper = sb("upper", [P, P], BF16)
        onesb = sb("onesb", [P, P], BF16)
        zerob = sb("zerob", [P, P], BF16)
        s48 = sb("s48", [G48, GH], F32)
        w1g = sb("w1g", [P, 4, GH], F32)
        w2g = sb("w2g", [G48, D], F32)
        b1g = sb("b1g", [P, GH], F32)
        b2g = sb("b2g", [P, D], F32)
        wr = sb("wr", [P, 4, NE], F32)
        brb = sb("brb", [P, NE], F32)
        initr = sb("initr", [P, ROW], F32)
        st = sb("st", [P, NT, 6], F32)
        ag = sb("ag", [P, NT, 2], F32)
        sm = sb("sm", [P, 6, NT], F32)
        valid = sb("valid", [P, NT], F32)
        iotae = sb("iotae", [P, NT, NE], F32)
        k128 = sb("k128", [P, NE, NT], F32)
        iotaj = sb("iotaj", [1, SLOTS, NE], F32)
        posi = sb("posi", [P, NT], I32)
        tei = sb("tei", [1, 32], I32)

        rt = sb("rt", [P, 6, NT, NE], F32)[:, :, :, :]
        pre = sb("pre", [P, 2, 18, NE], BF16)[:, :, :, :]
        ohb = sb("ohb", [P, NT, NE], BF16)[:, :, :]
        epre = sb("epre", [P, 2, 12], F32)[:, :, :]
        cmp_ = sb("cmp", [P, NE, NT], F32)[:, :, :]
        cmj = sb("cmj", [1, SLOTS, NE], F32)[:, :, :]
        tef = sb("tef", [1, 32], F32)[:, :]
        xn = sb("xn", [P, 2, D], F32)
        xnT = sb("xnT", [P, 2, D], F32)
        xs5 = sb("xs5", [P, SLOTS - 12, ROW], F32)

        def cut(region, n, cursor):
            a = region[:, cursor[0]:cursor[0] + n]
            cursor[0] += n
            return a

        late = mvr[:, :].bitcast(F32)
        at = [0]
        gsm = cut(late, 4 * NT * GH, at).rearrange("p (a q f) -> p a q f", a=4, q=NT)
        h3 = cut(late, NT * G48 // 2, at).bitcast(BF16).rearrange("p (q f) -> p q f", q=NT)
        aggT = cut(late, NT * P, at)
        hq = xs5[0:KE, :, :].rearrange("p j c -> p (j c)")[:, 0:NT * NC // 2].bitcast(BF16).rearrange("p (q c) -> p q c", q=NT)
        c1 = ct[1][:, :, :].rearrange("p q d -> p (q d)").bitcast(F32)
        at = [0]
        eI = cut(c1, 2 * NC, at)[0:KE, :].bitcast(I16).rearrange("p (a c two) -> p a c two", a=2, two=2)
        dI = cut(c1, 2 * EL, at)[0:NB // 2, :].bitcast(I32)
        mm = cut(c1, 4, at)[0:NB // 2, :].rearrange("p (a h) -> p a h", a=2)
        dg = cut(c1, 2 * NB, at)[0:NB // 2, :].rearrange("p (a b h) -> p a b h", a=2, h=2)
        at = [0]
        xs12 = cut(c1, 12 * ROW, at).rearrange("p (j c) -> p j c", j=12)
        c0 = ct[0][:, :, :].rearrange("p q d -> p (q d)").bitcast(F32)
        at = [0]
        hp = cut(c0, 2 * HID, at).rearrange("p (a h) -> p a h", a=2)
        hT = cut(c0, 2 * HID, at).rearrange("p (a h) -> p a h", a=2)
        yb = cut(c0, 4 * D, at).rearrange("p (a d) -> p a d", a=4)
        tw = xs5[0:KE, 0, 0:MS].bitcast(I16).rearrange("p (k two) -> p k two", two=2)
        K16 = xs5[0:KE, 1, 0:NC // 2].bitcast(I16)
        mvs = mvr[0:KE, :].rearrange("p (n a k c) -> p n a k c", n=RING, a=2, k=MS)

        def xs(j):
            return xs12[:, j, :] if j < 12 else xs5[:, j - 12, :]

        PS = [ctx.enter_context(nc.psum_tensor(f"ps{i}", [P, 512], F32)) for i in range(8)]
        pH = PS[6][:, 0:NT * GH].rearrange("p (q f) -> p q f", q=NT)
        pZ = PS[7][:, 0:NT * GH].rearrange("p (q f) -> p q f", q=NT)
        pBnd = PS[7][:, 0:2 * NB]
        pOut = PS[7][:, 0:NT]
        pBad = PS[5][0:1, 0:1]
        pDeg = PS[3][:, 0:NT]
        pA = [PS[4], PS[5], PS[2]]
        def window(b):
            return PS[b % PR][:, 0:MC]

        def turning(n):
            return PS[5] if n < NT else PS[4 + n % 2]

        def columns(b):
            return window(b).rearrange("p (q i) -> p q i", q=NT)

        ABLK = [(0, 512), (512, 1024), (1024, 1280)]
        pLg = PS[6][:, 0:NT * NE].rearrange("p (q e) -> p q e", q=NT)
        pRk = PS[7][:, 0:NT * NE].rearrange("p (q e) -> p q e", q=NT)
        pCn = PS[3][:, 0:NE]

        s_edge = sem("s_edge")
        s_x = [sem(f"s_xl{i}") for i in range(4)]
        s_gw = sem("s_gw")
        s_w1 = sem("s_w1")
        s_w2 = sem("s_w2")
        s_it = sem("s_it")
        s_init = sem("s_init")
        s_pad = sem("s_pad")
        s_cst = sem("s_cst")
        s_s48 = sem("s_s48")
        s_pl = sem("s_pl")
        s_dv = sem("s_dv")
        s_dg = sem("s_dg")
        s_bnd = sem("s_bnd")
        s_zc = sem("s_zc")
        s_base = sem("s_base")
        s_hq = sem("s_hq")
        s_bn = sem("s_bn")
        s_ba = sem("s_ba")
        s_nw = sem("s_nw")
        s_ve = sem("s_ve")
        s_sq = sem("s_sq")
        s_xn = sem("s_xn")
        s_xp = sem("s_xp")
        s_xe = sem("s_xe")
        s_h = sem("s_h")
        s_xb = sem("s_xb")
        s_gen = sem("s_gen")
        s_free = sem("s_free")
        s_blk = sem("s_blk")
        s_ev = sem("s_ev")
        s_car = sem("s_car")
        s_vio = sem("s_vio")
        s_bad = sem("s_bad")
        s_flag = sem("s_flag")
        s_sgen = sem("s_sgen")
        s_sfree = sem("s_sfree")
        s_swin = sem("s_swin")
        s_sc = sem("s_sc")
        s_sk = sem("s_sk")
        s_sdeg = sem("s_sdeg")
        s_sve = sem("s_sve")
        s_ssq = sem("s_ssq")
        s_deg = sem("s_deg")
        s_h3 = sem("s_h3")
        s_ag = sem("s_ag")
        s_age = sem("s_age")
        s_z = sem("s_z")
        s_o = sem("s_o")
        s_x1 = sem("s_x1")
        s_st = sem("s_st")
        s_oho = sem("s_oho")
        s_rk = sem("s_rk")
        s_pos = sem("s_pos")
        s_te = sem("s_te")
        s_scat = sem("s_scat")
        s_xs = [sem(f"s_xs{j}") for j in range(SLOTS)]
        s_f0 = sem("s_f0")
        s_ft = sem("s_ft")
        s_fx = sem("s_fx")
        s_fh = sem("s_fh")
        s_f1 = sem("s_f1")
        s_fp = sem("s_fp")
        s_fr = sem("s_fr")
        s_fy = sem("s_fy")
        s_f2 = sem("s_f2")
        s_out = [sem(f"s_out{i}") for i in range(4)]

        block = ctx.enter_context(nc.Block())

        def chain(eng, s):
            n = [0]

            def link(ins):
                n[0] += 1
                ins.then_inc(s, 1)
                eng.wait_ge(s, n[0])
            return link

        def bad(eng, name):
            r = eng.alloc_register(name)
            eng.wait_ge(s_flag, 1)
            eng.load([r], badI[0:1, 0:1])
            return r

        def places(eng, regs, b):
            eng.load(regs, baseI[0:1, b:b + len(regs)])
            return [eng.snap(r, min_val=0, max_val=N - 1) for r in regs]

        @block.sync
        def _(eng):
            eng.dma_start(eI.rearrange("p a c two -> p (a c two)").bitcast(I32), edges.rearrange("p a c -> p (a c)")).then_inc(s_edge, 16)
            eng.dma_start(dI, dst.rearrange("(b e) -> b e", b=NB // 2)).then_inc(s_edge, 16)
            eng.dma_start(w1g[:, :, :], gW1.rearrange("(k p) f -> p k f", p=P)).then_inc(s_gw, 16)
            eng.dma_start(b2g[:, :], gb2.rearrange("(a d) -> a d", a=1).broadcast_to([P, D])).then_inc(s_gw, 16)
            eng.dma_start(b1g[:, :], gb1.rearrange("(a d) -> a d", a=1).broadcast_to([P, GH])).then_inc(s_gw, 16)
            for i in range(3):
                eng.dma_start(w2g[i * GH:(i + 1) * GH, :], gW2).then_inc(s_gw, 16)
            eng.dma_start(wr[:, :, :], Wr.rearrange("(k p) e -> p k e", p=P)).then_inc(s_gw, 16)
            eng.dma_start(brb[:, :], br.rearrange("(a e) -> a e", a=1).broadcast_to([P, NE])).then_inc(s_gw, 16)
            for e in range(NE):
                eng.dma_start(w1[:, e, :, :], fW1[e].rearrange("(k p) h -> p k h", p=P)).then_inc(s_w1, 16)
            for e in range(NE):
                eng.dma_start(w2[:, e, :, :], fW2[e].rearrange("(k p) o -> p k o", p=P)).then_inc(s_w2, 16)
            eng.dma_start(b1t[:, :, :], fb1).then_inc(s_w2, 16)
            eng.dma_start(b2f[:, :, :], fb2.rearrange("(a e) o -> a e o", a=1).broadcast_to([P, NE, D])).then_inc(s_w2, 16)
            eng.wait_ge(s_it, 1)
            for j in range(SLOTS):
                eng.dma_start(routed[j * P:(j + 1) * P, :], initr[:, :]).then_inc(s_init, 16)
            eng.wait_ge(s_scat, 16 * NT)
            for j in range(SLOTS):
                eng.dma_start(xs(j), routed[j * P:(j + 1) * P, :]).then_inc(s_xs[j], 16)
            for i in range(4):
                eng.wait_ge(s_out[i], 16 * len(range(i, SLOTS, 4)))

        @block.gpsimd
        def _(eng):
            eng.memset(identf[:, :], 0.0).then_inc(s_pl, 1)
            eng.memset(onesf[:, :], 1.0).then_inc(s_pl, 1)
            eng.iota(ir2[:, :, :], [[1, P], [0, 2]], base=0, channel_multiplier=0).then_inc(s_cst, 1)
            eng.iota(im2[:, :, :], [[1, MC], [0, 2]], base=0, channel_multiplier=0).then_inc(s_cst, 1)
            eng.wait_ge(s_pl, 2)
            eng.affine_select(out=identf[:, :], in_=identf[:, :], compare_op=ALU.not_equal, fill=1.0,
                              base=0, pattern=[[-1, P]], channel_multiplier=1).then_inc(s_cst, 1)
            eng.memset(ct[0][:, 5:NT, :].rearrange("p q d -> p (q d)").bitcast(F32), 0.0).then_inc(s_zc, 1)
            eng.memset(initr[:, 0:D + 2], 0.0).then_inc(s_pl, 1)
            eng.memset(initr[:, D + 2:ROW].bitcast(I32), NOBODY).then_inc(s_it, 1)
            eng.memset(xt[:, :, D + 3:ROW], 0.0).then_inc(s_pl, 1)
            eng.memset(identb[:, :], 0.0).then_inc(s_pl, 1)
            eng.memset(onesb[:, :], 1.0).then_inc(s_pl, 1)
            eng.memset(zerob[:, :], 0.0).then_inc(s_pl, 1)
            eng.memset(s48[:, :], 0.0).then_inc(s_pl, 1)
            eng.memset(upper[:, :], 1.0).then_inc(s_pl, 1)
            eng.memset(valid[:, :], 1.0).then_inc(s_pl, 1)
            eng.wait_ge(s_pl, 10)
            eng.affine_select(out=identb[:, :], in_=identb[:, :], compare_op=ALU.not_equal, fill=1.0,
                              base=0, pattern=[[-1, P]], channel_multiplier=1).then_inc(s_cst, 1)
            eng.affine_select(out=upper[:, :], in_=upper[:, :], compare_op=ALU.is_gt, fill=0.0,
                              base=0, pattern=[[1, P]], channel_multiplier=-1).then_inc(s_cst, 1)
            eng.iota(iotae[:, :, :], [[0, NT], [1, NE]], base=0, channel_multiplier=0,
                     allow_small_or_imprecise_dtypes=True).then_inc(s_cst, 1)
            eng.iota(k128[:, :, :], [[0, NE], [P, NT]], base=0, channel_multiplier=0,
                     allow_small_or_imprecise_dtypes=True).then_inc(s_cst, 1)
            eng.iota(iotaj[:, :, :], [[1, SLOTS], [0, NE]], base=0, channel_multiplier=0,
                     allow_small_or_imprecise_dtypes=True).then_inc(s_cst, 1)
            eng.iota(xt[:, :, D + 2].bitcast(I32), [[P, NT]], base=0, channel_multiplier=1).then_inc(s_cst, 1)
            for i in range(3):
                eng.affine_select(out=s48[:, :], in_=s48[:, :], compare_op=ALU.not_equal, fill=1.0,
                                  base=-GH * i, pattern=[[-1, GH]], channel_multiplier=1).then_inc(s_s48, 1)
                eng.wait_ge(s_s48, i + 1)
            eng.affine_select(out=valid[:, :], in_=valid[:, :], compare_op=ALU.is_gt, fill=0.0,
                              base=N, pattern=[[-P, NT]], channel_multiplier=-1).then_inc(s_cst, 1)
            eng.wait_ge(s_gw, 16 * 8)
            eng.wait_ge(s_xn, NT)
            for q in range(NT):
                eng.tensor_tensor(xt[:, q, 0:D], xt[:, q, 0:D], b2g[:, :], ALU.add).then_inc(s_xb, 1)
            eng.wait_ge(s_init, 16 * SLOTS)
            eng.wait_ge(s_st, 2)
            eng.wait_ge(s_pos, 1)
            for q in range(NT):
                r = N - q * P if q == NT - 1 else P
                eng.indirect_dma_start(
                    out=routed, out_offset=bass.IndirectOffsetOnAxis(ap=posi[0:r, q:q + 1], axis=0),
                    in_=xt[0:r, q, :], in_offset=None).then_inc(s_scat, 16)
            for j in range(SLOTS):
                eng.wait_ge(s_f2, j + 1)
                eng.indirect_dma_start(
                    out=out, out_offset=bass.IndirectOffsetOnAxis(ap=xs(j)[:, D + 2:D + 3].bitcast(I32), axis=0),
                    in_=yb[:, j % 4, :], in_offset=None, bounds_check=N - 1, oob_is_err=False).then_inc(s_out[j % 4], 16)

        @block.scalar
        def _(eng):
            eng.wait_ge(s_pad, 1)
            for i in range(3):
                eng.dma_start(xt[:, 3 * i:3 * i + 3, 0:D],
                              x[3 * i * P:(3 * i + 3) * P, :].rearrange("(q p) d -> p q d", p=P)).then_inc(s_x[i], 16)
            eng.dma_start(xt[0:N - 9 * P, 9, 0:D], x[9 * P:N, :]).then_inc(s_x[3], 16)
            def transposed(q, n):
                eng.wait_ge(s_xp, n + 1)
                if n >= 2:
                    eng.wait_ge(s_h, n - 1)
                eng.activation(xnT[:, n % 2, :], turning(n)[:, :], ACT.Copy).then_inc(s_xe, 1)

            regs = [eng.alloc_register(f"act_b{i}") for i in range(8)]
            eng.wait_ge(s_zc, 2)
            eng.wait_ge(s_base, 1)
            for b in range(NB):
                if b % 8 == 0:
                    base = places(eng, regs, b)
                if b == GB * 14:
                    eng.wait_ge(s_ve, 1)
                    eng.activation(sm[:, 1, :], sm[:, 0, :], ACT.Sqrt).then_inc(s_sq, 1)
                q = b // GB - 22
                if b % GB == 0 and 0 <= q < NT:
                    eng.wait_ge(s_nw, 6)
                    if q >= 2:
                        eng.wait_ge(s_xp, q - 1)
                    eng.activation(xn[:, q % 2, :], xt[:, q, 0:D], ACT.Identity, scale=sm[:, 4, q:q + 1],
                                   bias=sm[:, 3, q:q + 1]).then_inc(s_xn, 1)
                if b % GB == 0 and 1 <= q <= NT:
                    transposed(q - 1, q - 1)
                eng.wait_ge(s_blk, b + 1)
                eng.wait_ge(s_ev, b)
                eng.activation(ct[0][:, :, bass.ds(base[b % 8] + 1, WD - 1)], columns(b)[:, :, 1:WD], ACT.Copy).then_inc(s_ev, 1)
            eng.wait_ge(s_ve, 2)
            eng.activation(sm[:, 1, :], sm[:, 0, :], ACT.Sqrt).then_inc(s_sq, 1)
            with eng.If_ne(bad(eng, "act_bad"), 0):
                eng.wait_ge(s_sve, 1)
                eng.activation(sm[:, 1, :], sm[:, 0, :], ACT.Sqrt).then_inc(s_ssq, 1)
            for layer in range(2):
                for i, (a, b) in enumerate(ABLK):
                    eng.wait_ge(s_ag, 3 * layer + i + 1)
                    eng.activation(aggT[0:G48, a:b], pA[i][0:G48, 0:b - a], ACT.Copy).then_inc(s_age, 1)
            for half in range(2):
                eng.wait_ge(s_ve, 3 + half)
                eng.activation(sm[:, 1, 0:5], sm[:, 0, 0:5], ACT.Sqrt).then_inc(s_sq, 1)
                eng.wait_ge(s_st, half + 1)
                for q in range(5 * half, 5 * half + 5):
                    n = NT + q
                    eng.wait_ge(s_xp, n - 1)
                    eng.activation(xn[:, q % 2, :], xt[:, q, 0:D], ACT.Identity, scale=xt[:, q, D:D + 1],
                                   bias=xt[:, q, D + 1:D + 2]).then_inc(s_xn, 1)
                    if q > 5 * half:
                        transposed(q - 1, n - 1)
                transposed(5 * half + 4, NT + 5 * half + 4)

            def routed_t(j):
                eng.wait_ge(s_ft, j + 1)
                if j == 0:
                    eng.wait_ge(s_h, 2 * NT)
                if j >= 2:
                    eng.wait_ge(s_fh, j - 1)
                eng.activation(xnT[:, j % 2, :], PS[j % 2][:, :], ACT.Copy).then_inc(s_fx, 1)

            def relu(j):
                eng.wait_ge(s_fp, j + 1)
                if j >= 2:
                    eng.wait_ge(s_fy, j - 1)
                for m in range(2):
                    last = eng.activation(hT[:, j % 2, m * P:(m + 1) * P], PS[4 + j % 2][:, m * P:(m + 1) * P],
                                          ACT.Relu, bias=b1t[:, m, ex[j]])
                last.then_inc(s_fr, 1)

            eng.wait_ge(s_te, 1)
            eng.wait_ge(s_w2, 16 * (NE + 2))
            ereg = [eng.alloc_register(f"act_e{j}") for j in range(SLOTS)]
            eng.load(ereg, tei[0:1, 0:SLOTS])
            ex = [bass.ds(eng.snap(r, min_val=0, max_val=NE - 1), 1) for r in ereg]
            routed_t(0)
            for j in range(SLOTS + 1):
                if j >= 1:
                    relu(j - 1)
                if j + 1 < SLOTS:
                    routed_t(j + 1)

        @block.tensor
        def _(eng):
            eng.wait_ge(s_cst, 3)
            eng.wait_ge(s_dg, 1)
            eng.matmul(pBnd, onesf[0:NB // 2, :], dg.rearrange("p a b h -> p (a b h)"), start=True, stop=True).then_inc(s_bnd, 1)

            def turned(n):
                eng.wait_ge(s_xn, n + 1)
                if n >= 1:
                    eng.wait_ge(s_xe, n if n < NT else n - 1)
                for k in range(4):
                    last = eng.transpose(turning(n)[:, k * P:(k + 1) * P], xn[:, n % 2, k * P:(k + 1) * P], identf[:, :])
                last.then_inc(s_xp, 1)

            def times(n, w, o):
                eng.wait_ge(s_xe, n + 1)
                for k in range(4):
                    last = eng.matmul(o, xnT[:, n % 2, k * P:(k + 1) * P], w[:, k, :], start=k == 0, stop=k == 3)
                last.then_inc(s_h, 1)

            for g in range(NG):
                eng.wait_ge(s_gen, g + 1)
                if g == 0:
                    eng.wait_ge(s_hq, 1)
                for i in range(GB):
                    b = GB * g + i
                    if b >= PR:
                        eng.wait_ge(s_car, b - PR + 1)
                    for c in range(2):
                        last = eng.matmul(window(b), oh[:, g % RING, i, :, c], mv[:, g % RING, i, :, c],
                                          start=c == 0, stop=c == 1)
                    last.then_inc(s_blk, 1)
                    for c in range(2):
                        last = eng.matmul(pOut, oh[:, g % RING, i, :, c], hq[:, :, 2 * b + c],
                                          start=b == 0 and c == 0, stop=b == NB - 1 and c == 1)
                last.then_inc(s_free, 1)
                q = g - 22
                if q == 0:
                    eng.wait_ge(s_gw, 16 * 8)
                if 0 <= q < NT:
                    turned(q)
                if 1 <= q <= NT:
                    times(q - 1, w1g, pH[:, q - 1, :])

            def degrees(cs):
                for k in range(NT):
                    for q in range(NT):
                        for c in cs:
                            last = eng.matmul(pDeg[:, k:k + 1], c[:, q, k * P:(k + 1) * P], onesb[:, 0:1],
                                              start=q == 0 and c is cs[0], stop=q == NT - 1 and c is cs[-1])
                return last

            eng.wait_ge(s_cst, 10)
            eng.wait_ge(s_ev, NB)
            eng.wait_ge(s_car, NB)
            degrees(ct[0:1]).then_inc(s_deg, 1)
            eng.wait_ge(s_vio, 1)
            eng.matmul(pBad, vio[:, NT:NT + 1], onesf[:, 0:1], start=True, stop=True).then_inc(s_bad, 1)
            flag = bad(eng, "pe_bad")
            with eng.If_ne(flag, 0):
                ps = PS[0]
                with eng.Fori(0, NWS) as t:
                    eng.wait_ge(s_sc, eng.snap(t * 3 + 1))
                    eng.matmul(ps[:, 0:2], zerob[:, :], onesb[:, 0:2], start=True, stop=True, skip_group_check=True)
                    with eng.Fori(0, NC // 4) as b:
                        n = eng.snap(t * (NC // 4) + b)
                        eng.wait_ge(s_sgen, n + 1)
                        for i in range(4):
                            last = eng.matmul(ps[:, 0:MS], oh[:, n % 2, i // 2, :, i % 2], mvs[:, n % 2, i // 2, :, i % 2],
                                              start=False, stop=True, skip_group_check=True)
                        last.then_inc(s_sfree, 1)
                    eng.matmul(ps[:, 0:2], zerob[:, :], onesb[:, 0:2], start=False, stop=True,
                               skip_group_check=True).then_inc(s_swin, 1)
                eng.wait_ge(s_sc, 3 * NWS + 1)
                degrees(ct).then_inc(s_sdeg, 1)

            def aggregate(cs):
                for i, (a, b) in enumerate(ABLK):
                    o = pA[i][0:G48, 0:b - a]
                    for q in range(NT):
                        for c in cs:
                            eng.matmul(o, h3[:, q, :], c[:, q, a:b], start=q == 0 and c is cs[0], stop=False)
                    for k in range(a // P, b // P):
                        last = eng.matmul(pA[i][0:G48, k * P - a:(k + 1) * P - a], h3[:, k, :], identb[:, :],
                                          start=False, stop=k == b // P - 1)
                    last.then_inc(s_ag, 1)

            for layer in range(2):
                eng.wait_ge(s_h3, layer + 1)
                with eng.If_ne(flag, 0):
                    aggregate(ct)
                with eng.Else():
                    aggregate(ct[0:1])
                for k in range(NT):
                    eng.wait_ge(s_age, 3 * layer + 1 + k // 4)
                    if layer == 0:
                        last = eng.matmul(pZ[:, k, :], aggT[0:G48, k * P:(k + 1) * P], s48[:, :], start=True, stop=True)
                    else:
                        if k >= 2:
                            eng.wait_ge(s_x1, k - 1)
                        eng.matmul(PS[k % 2][:, :], aggT[0:G48, k * P:(k + 1) * P], w2g[:, :], start=True, stop=True)\
                           .then_inc(s_o, 1)
                if layer == 0:
                    last.then_inc(s_z, 1)

            for q in range(NT):
                turned(NT + q)
                if q >= 1:
                    times(NT + q - 1, wr, pLg[:, q - 1, :])
            times(2 * NT - 1, wr, pLg[:, NT - 1, :])
            eng.wait_ge(s_oho, 1)
            eng.matmul(PS[7][:, 0:NT * NE], upper[:, :], ohb, start=True, stop=False)
            eng.matmul(PS[7][:, 0:NT * NE], onesb[:, :], pre[:, 0, 7:17, :], start=False, stop=True)
            eng.matmul(pCn, onesb[:, :], pre[:, 0, 17, :], start=True, stop=True).then_inc(s_rk, 1)

            def feed(j):
                eng.wait_ge(s_f0, j + 1)
                if j >= 2:
                    eng.wait_ge(s_fx, j - 1)
                for k in range(4):
                    last = eng.transpose(PS[j % 2][:, k * P:(k + 1) * P], xn[:, j % 2, k * P:(k + 1) * P], identf[:, :])
                last.then_inc(s_ft, 1)

            def up(j):
                eng.wait_ge(s_fx, j + 1)
                if j >= 2:
                    eng.wait_ge(s_f1, j - 1)
                for k in range(4):
                    last = eng.matmul(PS[2 + j % 2][:, 0:HID], xnT[:, j % 2, k * P:(k + 1) * P], w1[:, ex[j], k, :],
                                      start=k == 0, stop=k == 3)
                last.then_inc(s_fh, 1)

            def turn(j):
                eng.wait_ge(s_f1, j + 1)
                if j >= 2:
                    eng.wait_ge(s_fr, j - 1)
                for k in range(2):
                    last = eng.transpose(PS[4 + j % 2][:, k * P:(k + 1) * P], hp[:, j % 2, k * P:(k + 1) * P], identf[:, :])
                last.then_inc(s_fp, 1)

            def down(j):
                eng.wait_ge(s_fr, j + 1)
                if j >= 2:
                    eng.wait_ge(s_f2, j - 1)
                for k in range(2):
                    last = eng.matmul(PS[6 + j % 2][:, :], hT[:, j % 2, k * P:(k + 1) * P], w2[:, ex[j], k, :],
                                      start=k == 0, stop=k == 1)
                last.then_inc(s_fy, 1)

            eng.wait_ge(s_te, 1)
            eng.wait_ge(s_w1, 16 * NE)
            eng.wait_ge(s_w2, 16 * (NE + 2))
            ereg = [eng.alloc_register(f"pe_e{j}") for j in range(SLOTS)]
            eng.load(ereg, tei[0:1, 0:SLOTS])
            ex = [eng.snap(r, min_val=0, max_val=NE - 1) for r in ereg]
            feed(0)
            for j in range(SLOTS + 1):
                if j < SLOTS:
                    up(j)
                if j >= 1:
                    turn(j - 1)
                if j + 1 < SLOTS:
                    feed(j + 1)
                if j >= 1:
                    down(j - 1)

        @block.vector
        def _(eng):
            link = chain(eng, s_dv)

            eng.memset(xt[96:P, NT - 1, 0:D], 0.0).then_inc(s_pad, 1)
            eng.memset(ct[0][:, 0:5, :].rearrange("p q d -> p (q d)").bitcast(F32), 0.0).then_inc(s_zc, 1)
            eng.wait_ge(s_edge, 32)
            sI, tI = eI[:, 0, :, 0], eI[:, 1, :, 0]
            dv = dI.rearrange("p (h e) -> p h e", h=2)
            link(eng.tensor_reduce(mm[:, 0, :], dv, X, ALU.min))
            link(eng.tensor_reduce(mm[:, 1, :], dv, X, ALU.max))
            eng.wait_ge(s_cst, 3)
            shape = [NB // 2, NB // 2, 2]
            for a in range(2):
                ins = eng.tensor_tensor(dg[:, a, :, :], identf[0:NB // 2, 0:NB // 2].unsqueeze(2).to_broadcast(shape),
                                        mm[:, a, :].unsqueeze(1).to_broadcast(shape), ALU.mult)
                if a == 0:
                    link(ins)
                else:
                    ins.then_inc(s_dg, 1)
            link(eng.tensor_scalar(R16[:, :], sI, P - 1, None, ALU.bitwise_and))
            link(eng.tensor_scalar(Q16[:, :], sI, 7, None, ALU.logical_shift_right))
            link(eng.tensor_copy(D16[:, :], tI))
            link(eng.scalar_tensor_tensor(out=G16[:, :], in0=Q16[:, :], scalar=float(WD), in1=D16[:, :],
                                          op0=ALU.mult, op1=ALU.add))
            for q in range(NT):
                last = eng.tensor_scalar(hq[:, q, :], Q16[:, :], q, None, ALU.is_equal)
            last.then_inc(s_hq, 1)
            eng.wait_ge(s_bnd, 1)
            gv = G16[:, :].rearrange("p (b c) -> p b c", c=2)
            link(eng.tensor_tensor(gv, gv, pBnd[0:KE, 0:NB].unsqueeze(2).to_broadcast([KE, NB, 2]), ALU.subtract))
            link(eng.tensor_copy(row[:, :, :], pBnd[0:1, :].rearrange("p (a b) -> p a b", a=2)))
            gap = rt[0:1, :, :, :].rearrange("p a q e -> p (a q e)")
            link(eng.tensor_tensor(gap[:, 0:NB - 1], row[:, 1, 0:NB - 1], row[:, 0, 1:NB], ALU.subtract))
            link(eng.tensor_reduce(wl[:, 0:1], gap[:, 0:NB - 1], X, ALU.max))
            link(eng.tensor_scalar(wl[:, 1:2], wl[:, 0:1], 0.0, None, ALU.is_le))
            eng.tensor_scalar(baseI[:, :], row[:, 0, :], wl[:, 1:2], None, ALU.mult).then_inc(s_base, 1)

            def stats(q):
                link(eng.bn_stats(st[:, q, :], xt[:, q, 0:D]))
                link(eng.bn_aggr(ag[:, q, :], st[:, q, :]))

            def newton(r, n, link):
                v, s, a = sm[:, 0, 0:n], sm[:, 1, 0:n], sm[:, 2, 0:n]
                y = sm[:, 3, 0:n]
                link(eng.reciprocal(y, s))
                link(eng.tensor_tensor(a, y, y, ALU.mult))
                link(eng.tensor_tensor(a, a, v, ALU.mult))
                link(eng.tensor_scalar(a, a, -0.5, 1.5, ALU.mult, ALU.add))
                link(eng.tensor_tensor(r, y, a, ALU.mult))

            v, s, a, y, r = (sm[:, i, :] for i in (0, 1, 2, 3, 4))
            first = [lambda: eng.reciprocal(y, s),
                     lambda: eng.tensor_tensor(a, y, y, ALU.mult),
                     lambda: eng.tensor_tensor(a, a, v, ALU.mult),
                     lambda: eng.tensor_scalar(a, a, -0.5, 1.5, ALU.mult, ALU.add),
                     lambda: eng.tensor_tensor(r, y, a, ALU.mult),
                     lambda: eng.scalar_tensor_tensor(out=y, in0=ag[:, :, 0], scalar=-1.0, in1=r, op0=ALU.mult, op1=ALU.mult)]
            regs = [eng.alloc_register(f"dve_b{i}") for i in range(8)]
            base = [None]

            def carry(b):
                if b % 8 == 0:
                    base[0] = places(eng, regs, b)
                eng.wait_ge(s_ev, b + 1)
                eng.wait_ge(s_car, b)
                col = ct[0][:, :, bass.ds(base[0][b % 8], 1)]
                eng.tensor_tensor(col, col, columns(b)[:, :, 0:1], ALU.add).then_inc(s_car, 1)

            def onehot(g, o, w, i2, k, at, n):
                b = GB * g + at
                return eng.tensor_tensor(
                    o[:, g % RING, at:at + n], i2[:, :, :].unsqueeze(1).to_broadcast([KE, n, w, 2]),
                    k[:, 2 * b:2 * (b + n)].rearrange("p (b c) -> p b c", c=2).unsqueeze(2).to_broadcast([KE, n, w, 2]),
                    ALU.is_equal)

            eng.wait_ge(s_pad, 1)
            eng.wait_ge(s_zc, 2)
            eng.wait_ge(s_base, 1)
            for g in range(NG + 2):
                if g < NG:
                    if g >= RING:
                        eng.wait_ge(s_free, g - RING + 1)
                    onehot(g, oh, P, ir2, R16, 0, GB)
                b = GB * (g - 2)
                if b >= 0:
                    carry(b)
                if g < NG:
                    onehot(g, mv, MC, im2, G16, 0, 2)
                if b >= 0:
                    carry(b + 1)
                if g < NG:
                    onehot(g, mv, MC, im2, G16, 2, 2).then_inc(s_gen, 1)
                if b >= 0:
                    carry(b + 2)
                    carry(b + 3)
                q = g - 3
                if 0 <= q < NT:
                    if q % 3 == 0:
                        eng.wait_ge(s_x[q // 3], 16)
                    eng.bn_stats(st[:, q, :], xt[:, q, 0:D]).then_inc(s_bn, 1)
                if 1 <= q <= NT:
                    eng.wait_ge(s_bn, q)
                    eng.bn_aggr(ag[:, q - 1, :], st[:, q - 1, :]).then_inc(s_ba, 1)
                if q == NT + 1:
                    eng.wait_ge(s_ba, NT)
                    eng.tensor_scalar(sm[:, 0, :], ag[:, :, 1], EPS, None, ALU.add).then_inc(s_ve, 1)
                k = g - 16
                if 0 <= k < len(first):
                    eng.wait_ge(s_sq, 1)
                    eng.wait_ge(s_nw, k)
                    first[k]().then_inc(s_nw, 1)

            eng.wait_ge(s_cst, 10)
            eng.wait_ge(s_free, NG)
            link(eng.tensor_scalar(vio[:, 0:NT], pOut, 256.0, None, ALU.is_gt))
            eng.tensor_reduce(vio[:, NT:NT + 1], vio[:, 0:NT], X, ALU.max).then_inc(s_vio, 1)
            link(eng.tensor_tensor(gap[:, 0:NB], row[:, 1, :], row[:, 0, :], ALU.subtract))
            link(eng.tensor_reduce(wl[:, 2:3], gap[:, 0:NB], X, ALU.max))
            link(eng.tensor_scalar(wl[:, 3:4], wl[:, 2:3], float(WD), None, ALU.is_ge))
            link(eng.tensor_tensor(wl[:, 4:5], wl[:, 3:4], wl[:, 1:2], ALU.subtract))
            eng.wait_ge(s_deg, 1)
            eng.tensor_scalar(sm[:, 0, :], pDeg, 1.0, None, ALU.add).then_inc(s_ve, 1)
            eng.wait_ge(s_bad, 1)
            eng.tensor_scalar(badI[:, 0:1], pBad, wl[:, 4:5], 1.0, ALU.add, ALU.add).then_inc(s_flag, 1)
            flag = bad(eng, "dve_bad")
            eng.wait_ge(s_sq, 2)
            dinv = sm[:, 5, :]
            newton(dinv, NT, link)
            with eng.If_ne(flag, 0):
                slink = chain(eng, s_sk)
                slink(eng.scalar_tensor_tensor(out=K16, in0=D16[:, :], scalar=float(NT), in1=Q16[:, :],
                                               op0=ALU.mult, op1=ALU.add))
                slink(eng.tensor_copy(tw[:, 0:MC, :], im2[:, :, :]))
                slink(eng.tensor_scalar(tw[:, MC:MS, :], im2[:, :, :], float(MC), None, ALU.add))
                eng.sem_inc(s_sfree, 2)
                eng.sem_inc(s_sc, 1)
                with eng.Fori(0, NWS) as t:
                    with eng.Fori(0, NC // 4) as b:
                        n = eng.snap(t * (NC // 4) + b)
                        eng.wait_ge(s_sfree, n + 1)
                        for o, w, i2, k in ((oh[:, n % 2, 0:2], P, ir2, R16), (mvs[:, n % 2], MS, tw, K16)):
                            last = eng.tensor_tensor(
                                o, i2[:, :, :].unsqueeze(1).to_broadcast([KE, 2, w, 2]),
                                k[:, bass.ds(b * 4, 4)].rearrange("p (b c) -> p b c", c=2).unsqueeze(2).to_broadcast([KE, 2, w, 2]),
                                ALU.is_equal)
                        last.then_inc(s_sgen, 1)
                    eng.wait_ge(s_sgen, eng.snap(t * (NC // 4) + NC // 4))
                    eng.tensor_scalar(tw[:, :, :], tw[:, :, :], float(MS), None, ALU.add).then_inc(s_sc, 1)
                    eng.wait_ge(s_swin, t + 1)
                    p = PS[0][:, 0:MS].rearrange("p (i q) -> p q i", q=NT)
                    to = bass.ds(t * WS, WS)
                    eng.tensor_copy(ct[0][:, :, to], p).then_inc(s_sc, 1)
                    eng.wait_ge(s_sc, eng.snap(t * 3 + 3))
                    eng.tensor_tensor(ct[1][:, :, to], p, ct[0][:, :, to], ALU.subtract).then_inc(s_sc, 1)
                eng.wait_ge(s_sdeg, 1)
                eng.tensor_scalar(sm[:, 0, :], pDeg, 1.0, None, ALU.add).then_inc(s_sve, 1)
                eng.wait_ge(s_ssq, 1)
                newton(dinv, NT, slink)
            db = dinv.unsqueeze(2).to_broadcast([P, NT, GH])

            def split(a):
                link(eng.tensor_copy(h3[:, :, 0:GH], a))
                link(eng.tensor_tensor(gsm[:, 1], a, h3[:, :, 0:GH], ALU.subtract))
                link(eng.tensor_copy(h3[:, :, GH:2 * GH], gsm[:, 1]))
                eng.tensor_tensor(h3[:, :, 2 * GH:G48], gsm[:, 1], h3[:, :, GH:2 * GH], ALU.subtract).then_inc(s_h3, 1)

            eng.wait_ge(s_h, NT)
            link(eng.tensor_tensor(gsm[:, 0], pH, db, ALU.mult))
            split(gsm[:, 0])
            eng.wait_ge(s_z, 1)
            link(eng.tensor_tensor(gsm[:, 2], pZ, db, ALU.mult))
            link(eng.tensor_tensor(gsm[:, 3], gsm[:, 2], b1g[:, :].unsqueeze(1).to_broadcast([P, NT, GH]), ALU.add))
            link(eng.scalar_tensor_tensor(out=gsm[:, 0], in0=gsm[:, 3], scalar=0.0, in1=db, op0=ALU.max, op1=ALU.mult))
            split(gsm[:, 0])

            eng.wait_ge(s_xb, NT)
            for half in range(2):
                qs = slice(5 * half, 5 * half + 5)
                for q in range(5 * half, 5 * half + 5):
                    eng.wait_ge(s_o, q + 1)
                    eng.scalar_tensor_tensor(out=xt[:, q, 0:D], in0=PS[q % 2][:, :], scalar=dinv[:, q:q + 1],
                                             in1=xt[:, q, 0:D], op0=ALU.mult, op1=ALU.add).then_inc(s_x1, 1)
                    eng.wait_ge(s_x1, q + 1)
                    stats(q)
                eng.tensor_scalar(sm[:, 0, 0:5], ag[:, qs, 1], EPS, None, ALU.add).then_inc(s_ve, 1)
                eng.wait_ge(s_sq, 3 + half)
                newton(xt[:, qs, D], 5, link)
                eng.scalar_tensor_tensor(out=xt[:, qs, D + 1], in0=ag[:, qs, 0], scalar=-1.0, in1=xt[:, qs, D],
                                         op0=ALU.mult, op1=ALU.mult).then_inc(s_st, 1)

            for i in range(2):
                link(eng.memset(pre[:, i, 0:8, :], 0.0))
                link(eng.memset(epre[:, i, 0:4], 0.0))
            eng.wait_ge(s_h, 2 * NT)
            link(eng.tensor_tensor(rt[:, 0], pLg, brb[:, :].unsqueeze(1).to_broadcast([P, NT, NE]), ALU.add))
            link(eng.tensor_reduce(sm[:, 2, :], rt[:, 0], X, ALU.max))
            link(eng.tensor_tensor(rt[:, 1], rt[:, 0], sm[:, 2, :].unsqueeze(2).to_broadcast([P, NT, NE]), ALU.is_equal))
            link(eng.scalar_tensor_tensor(out=rt[:, 2], in0=rt[:, 1], scalar=-float(NE), in1=iotae[:, :, :],
                                          op0=ALU.mult, op1=ALU.add))
            link(eng.tensor_reduce(sm[:, 3, :], rt[:, 2], X, ALU.min))
            link(eng.tensor_tensor(rt[:, 1], rt[:, 2], sm[:, 3, :].unsqueeze(2).to_broadcast([P, NT, NE]), ALU.is_equal))
            link(eng.tensor_tensor(rt[:, 3], rt[:, 1], valid[:, :].unsqueeze(2).to_broadcast([P, NT, NE]), ALU.mult))
            link(eng.tensor_copy(ohb, rt[:, 3]))
            link(eng.tensor_copy(pre[:, 0, 8:18, :], rt[:, 3]))
            for i, s in enumerate((1, 2, 4, 8)):
                ins = eng.tensor_tensor(pre[:, 1 - i % 2, 8:18, :], pre[:, i % 2, 8:18, :], pre[:, i % 2, 8 - s:18 - s, :], ALU.add)
                if s < 8:
                    link(ins)
                else:
                    ins.then_inc(s_oho, 1)
            eng.wait_ge(s_rk, 1)
            link(eng.tensor_tensor(cmp_, pCn.unsqueeze(2).to_broadcast([P, NE, NT]), k128[:, :, :], ALU.is_gt))
            link(eng.tensor_reduce(epre[:, 0, 4:12], cmp_, X, ALU.add))
            for i, s in enumerate((1, 2, 4)):
                link(eng.tensor_tensor(epre[:, 1 - i % 2, 4:12], epre[:, i % 2, 4:12], epre[:, i % 2, 4 - s:12 - s], ALU.add))
            link(eng.scalar_tensor_tensor(out=rt[:, 4], in0=epre[:, 1, 3:11].unsqueeze(1).to_broadcast([P, NT, NE]),
                                          scalar=float(P), in1=pRk, op0=ALU.mult, op1=ALU.add))
            link(eng.tensor_tensor(rt[:, 5], rt[:, 4], rt[:, 3], ALU.mult))
            link(eng.tensor_reduce(sm[:, 2, :], rt[:, 5], X, ALU.add))
            eng.tensor_copy(posi[:, :], sm[:, 2, :]).then_inc(s_pos, 1)
            link(eng.tensor_tensor(cmj[0:1], epre[0:1, 1, 4:12].unsqueeze(1).to_broadcast([1, SLOTS, NE]),
                                   iotaj[:, :, :], ALU.is_le))
            link(eng.tensor_reduce(tef[0:1, 0:SLOTS], cmj[0:1], X, ALU.add))
            link(eng.tensor_scalar(tef[0:1, 0:SLOTS], tef[0:1, 0:SLOTS], float(NE - 1), None, ALU.min))
            eng.tensor_copy(tei[:, 0:SLOTS], tef[0:1, 0:SLOTS]).then_inc(s_te, 1)
            eng.wait_ge(s_te, 1)
            ereg = [eng.alloc_register(f"dve_e{j}") for j in range(SLOTS)]
            eng.load(ereg, tei[0:1, 0:SLOTS])
            ex = [eng.snap(r, min_val=0, max_val=NE - 1) for r in ereg]

            def ready(j):
                eng.wait_ge(s_xs[j], 16)
                if j >= 2:
                    eng.wait_ge(s_ft, j - 1)
                eng.tensor_scalar(xn[:, j % 2, :], xs(j)[:, 0:D], xs(j)[:, D:D + 1], xs(j)[:, D + 1:D + 2],
                                  ALU.mult, ALU.add).then_inc(s_f0, 1)

            def hidden(j):
                eng.wait_ge(s_fh, j + 1)
                if j >= 2:
                    eng.wait_ge(s_fp, j - 1)
                eng.tensor_copy(hp[:, j % 2, :], PS[2 + j % 2][:, 0:HID]).then_inc(s_f1, 1)

            def final(j):
                eng.wait_ge(s_fy, j + 1)
                if j >= 4:
                    eng.wait_ge(s_out[j % 4], 16 * (j // 4))
                y = yb[:, j % 4, :]
                link(eng.tensor_tensor(y, PS[6 + j % 2][:, :], b2f[:, ex[j], :], ALU.add))
                eng.tensor_tensor(y, y, xs(j)[:, 0:D], ALU.add).then_inc(s_f2, 1)

            eng.wait_ge(s_w2, 16 * (NE + 2))
            ready(0)
            ready(1)
            for j in range(SLOTS + 1):
                if j < SLOTS:
                    hidden(j)
                if j + 2 < SLOTS:
                    ready(j + 2)
                if j >= 1:
                    final(j - 1)


_INS = ["x", "src", "dst", "L0_gnn_W1", "L0_gnn_b1", "L0_gnn_W2", "L0_gnn_b2", "L0_ffn_Wr", "L0_ffn_br",
        "L0_ffn_W1", "L0_ffn_b1", "L0_ffn_W2", "L0_ffn_b2"]


def kernel(**inputs):
    import numpy as _np
    import concourse.bacc as _bacc
    from concourse import mybir as _mybir
    from concourse.bass_utils import run_bass_kernel_spmd as _run

    nc = _bacc.Bacc("TRN2", target_bir_lowering=False, num_devices=1)
    arrays, args = {}, []
    for name in _INS:
        a = _np.ascontiguousarray(inputs[name])
        if name == "src":
            e = _np.stack([a, _np.asarray(inputs["dst"])]).reshape(2, NC, KE)
            a = _np.ascontiguousarray(e.transpose(2, 0, 1))
        elif name == "L0_ffn_b1":
            a = _np.ascontiguousarray(a.reshape(NE, 2, P).transpose(2, 1, 0))
        arrays[f"in_{name}"] = a
        args.append(nc.dram_tensor(f"in_{name}", a.shape, _mybir.dt.from_np(a.dtype), kind="ExternalInput").ap())
    args.append(nc.dram_tensor("out_0", (N, D), F32, kind="ExternalOutput").ap())
    program(nc, *args)
    r = _run(nc, [arrays], core_ids=[0])
    return r.results[0]["out_0"]
```

```python
import concourse.bass as bass
from concourse import mybir
from contextlib import ExitStack, nullcontext

F32 = mybir.dt.float32
BF16 = mybir.dt.bfloat16
I16 = mybir.dt.int16
I32 = mybir.dt.int32
ALU = mybir.AluOpType
ACT = mybir.ActivationFunctionType
X = mybir.AxisListType.X

N = 1250
D = 512
P = 128
NT = 10
TAIL = N - (NT - 1) * P
NC, KE = 320, 125
NB, GB = NC // 2, 4
NG, GC = NB // GB, 2 * GB
WD = 12
MC = NT * WD
WIDTH = [8] * (NG // 2) + [10] * (NG // 4) + [WD] * (NG // 4)
SPANS = [8] * (NC // 16) + [4] * (NC // 8)
NS = len(SPANS)
SW = 42
CW = NT * P + SW
MANY = 32
RING = 4
XB = 56
LAG = 3
PR = 6
SROWS = 80
WS = 40
NWS, MS = NT * P // WS, NT * WS
NE, HID = 8, 256
SLOTS = (N - NE) // P + NE
ROW = D + 4
NOBODY = 1 << 20
EPS = 1e-5
GH = 16
G48 = 3 * GH
WC = GH + 8


def program(nc, x, edges, order, ends, bases, gW1, gb1, gW2, gb2, Wr, br, fW1, fb1, fW2, fb2, out):
    ctx = ExitStack()
    with ctx:
        def sb(name, shape, dt):
            return ctx.enter_context(nc.sbuf_tensor(name, shape, dt))

        def sem(name):
            return ctx.enter_context(nc.semaphore(name))

        routed = nc.dram_tensor("routed", [SLOTS * P, ROW], F32, kind="Internal").ap()

        xt = sb("xt", [P, NT, ROW], F32)
        w1 = sb("w1", [P, NE, 4, HID], F32)
        w2 = sb("w2", [P, NE, 2, D], F32)
        b1t = sb("b1t", [P, 2, NE], F32)
        b2f = sb("b2f", [P, NE, D], F32)
        ct = [sb("ct0", [P, NT, CW], BF16), sb("ct1", [P, NT, NT * P], BF16)]
        oh = sb("oh", [KE, RING, GB, P, 2], BF16)
        mvr = sb("mv", [P, 4800], BF16)
        mv = mvr[0:KE, 0:RING * GB * MC * 2].rearrange("p (n k) -> p n k", n=RING)
        ir2 = sb("ir2", [KE, P, 2], I16)
        im2 = {w: sb(f"im{w}", [KE, NT * w, 2], I16) for w in (8, 10, WD)}
        R16 = sb("R16", [KE, NC], I16)
        Q16 = sb("Q16", [KE, NC], I16)
        G16 = sb("G16", [KE, NC], I16)
        badI = sb("badI", [1, 2], I32)
        vio = sb("vio", [P, 1], F32)
        most = sb("most", [P, 2, NS], F32)
        odd = sb("odd", [P, 3], F32)
        onesf = sb("onesf", [P, P], F32)
        identf = sb("identf", [P, P], F32)
        identb = sb("identb", [P, P], BF16)
        upper = sb("upper", [P, P], BF16)
        onesb = sb("onesb", [P, P], BF16)
        zerob = sb("zerob", [P, P], BF16)
        zeros = zerob[:, 0:1].to_broadcast([P, NT * SW])
        w0 = sb("w0", [P, 4, WC], F32)
        wc = sb("wc", [P, 4, WC], F32)
        w2t = sb("w2t", [P, 4, G48 + 1], F32)
        wb = sb("wb", [P, 4, NE], F32)
        wz = sb("wz", [G48, NE], F32)
        bz = sb("bz", [P, NE], F32)
        xr = sb("xr", [P, NT, NE], F32)
        w2g = sb("w2g", [G48 + 1, D], F32)
        b1g = sb("b1g", [P, GH], F32)
        b2g = sb("b2g", [P, D], F32)
        brb = sb("brb", [P, NE], F32)
        initr = sb("initr", [P, ROW], F32)
        st = sb("st", [P, NT, 6], F32)
        ag = sb("ag", [P, NT, 2], F32)
        sm = sb("sm", [P, 6, NT], F32)
        valid = sb("valid", [P, NT], F32)
        iotae = sb("iotae", [P, NT, NE], F32)
        k128 = sb("k128", [P, NE, NT], F32)
        iotaj = sb("iotaj", [1, SLOTS, NE], F32)
        posi = sb("posi", [P, NT], I32)
        tei = sb("tei", [1, 32], I32)

        rt = sb("rt", [P, 6, NT, NE], F32)[:, :, :, :]
        pre = sb("pre", [P, 2, 18, NE], BF16)[:, :, :, :]
        ohb = sb("ohb", [P, NT, NE], BF16)[:, :, :]
        epre = sb("epre", [P, 2, 12], F32)[:, :, :]
        cmp_ = sb("cmp", [P, NE, NT], F32)[:, :, :]
        cmj = sb("cmj", [1, SLOTS, NE], F32)[:, :, :]
        tef = sb("tef", [1, 32], F32)[:, :]
        xn = sb("xn", [P, 2, D], F32)
        xnT = sb("xnT", [P, 2, D], F32)
        xs5 = sb("xs5", [P, SLOTS - 12, ROW], F32)

        def cut(region, n, cursor):
            a = region[:, cursor[0]:cursor[0] + n]
            cursor[0] += n
            return a

        late = mvr[:, :].bitcast(F32)
        at = [0]
        gsm = cut(late, 4 * NT * GH, at).rearrange("p (a q f) -> p a q f", a=4, q=NT)
        h3 = cut(late, NT * G48 // 2, at).bitcast(BF16).rearrange("p (q f) -> p q f", q=NT)
        aggT = cut(late, NT * P, at)
        c1 = ct[1][:, :, :].rearrange("p q d -> p (q d)").bitcast(F32)
        at = [0]
        eI = cut(c1, 2 * NC, at)[0:KE, :].bitcast(I16).rearrange("p (a c two) -> p a c two", a=2, two=2)
        dI = cut(c1, 501, at)[0:SROWS, :].bitcast(I32)
        bnd = cut(c1, NC, at).bitcast(I32)
        ends3 = cut(c1, 3 * NC, at)[0:1, :].bitcast(I32).rearrange("p (a c) -> p a c", a=3)
        ends3f = cut(c1, 3 * NC, at)[0:1, :].rearrange("p (a c) -> p a c", a=3)
        off, spn, lim = (cut(c1, NC, at)[0:1, :] for _ in range(3))
        offI = cut(c1, NC, at)[0:1, :].bitcast(I32)
        begin = cut(c1, NS, at)[0:1, :].bitcast(I32)
        baseI = cut(c1, NS, at)[0:1, :].bitcast(I32)
        back = cut(c1, NS, at)[0:1, :]
        wl = cut(c1, 2, at)[0:1, :]
        unord = cut(c1, 500, at)[0:SROWS, :]
        inrow = cut(c1, 501, at)[0:SROWS, :]
        top = cut(c1, 4, at)
        at = [0]
        xs12 = cut(c1, 12 * ROW, at).rearrange("p (j c) -> p j c", j=12)
        c0 = ct[0][:, :, :].rearrange("p q d -> p (q d)").bitcast(F32)
        at = [0]
        w1c = cut(c0, 8 * HID, at).rearrange("p (a k h) -> p a k h", a=2, k=4)
        hT = cut(c0, 2 * HID, at).rearrange("p (a h) -> p a h", a=2)
        yb = cut(c0, 4 * D, at).rearrange("p (a d) -> p a d", a=4)
        tw = xs5[0:KE, 0, 0:MS].bitcast(I16).rearrange("p (k two) -> p k two", two=2)
        K16 = xs5[0:KE, 1, 0:NC // 2].bitcast(I16)
        mvs = mvr[0:KE, 0:4 * MS * 2].rearrange("p (n a k c) -> p n a k c", a=2, k=MS, c=2)

        def xs(j):
            return xs12[:, j, :] if j < 12 else xs5[:, j - 12, :]

        PS = [ctx.enter_context(nc.psum_tensor(f"ps{i}", [P, 512], F32)) for i in range(8)]
        pH = PS[6][:, 0:NT * WC].rearrange("p (q f) -> p q f", q=NT)
        pCs = PS[6][:, 0:WC]
        pWz = PS[6][0:G48, 0:NE]
        pBz = PS[6][:, NE:2 * NE]
        pX = [PS[0], PS[1], PS[3], PS[7]]
        pZ = PS[7][:, 0:NT * G48].rearrange("p (q f) -> p q f", q=NT)
        pBad = PS[5][0:1, 0:1]
        pDeg = PS[3][:, 0:NT]
        pA = [PS[4], PS[5], PS[2]]
        def bank(s):
            return PS[(0, 1, 2, 3, 4, 7)[s % PR]][:, 0:NT * SW]

        def span(s):
            return bank(s).rearrange("p (q i) -> p q i", q=NT)

        ABLK = [(0, 512), (512, 1024), (1024, 1280)]
        pLg = PS[6][:, 0:NT * NE].rearrange("p (q e) -> p q e", q=NT)
        pRk = PS[7][:, 0:NT * NE].rearrange("p (q e) -> p q e", q=NT)
        pCn = PS[3][:, 0:NE]

        s_edge = sem("s_edge")
        s_place = sem("s_place")
        s_sp = sem("s_sp")
        s_ord = sem("s_ord")
        s_end = sem("s_end")
        s_x = [sem(f"s_xl{i}") for i in range(4)]
        s_gw = sem("s_gw")
        s_w1 = sem("s_w1")
        s_w2 = sem("s_w2")
        s_it = sem("s_it")
        s_init = sem("s_init")
        s_pad = sem("s_pad")
        s_cst = sem("s_cst")
        s_pl = sem("s_pl")
        s_dv = sem("s_dv")
        s_key = sem("s_key")
        s_pl2 = sem("s_pl2")
        s_zc = sem("s_zc")
        s_zero = sem("s_zero")
        s_base = sem("s_base")
        s_bn = sem("s_bn")
        s_ba = sem("s_ba")
        s_nw = sem("s_nw")
        s_cs = sem("s_cs")
        s_w2t = sem("s_w2t")
        s_wc = sem("s_wc")
        s_wz = sem("s_wz")
        s_xr = sem("s_xr")
        s_ve = sem("s_ve")
        s_sq = sem("s_sq")
        s_xp = sem("s_xp")
        s_xe = sem("s_xe")
        s_h = sem("s_h")
        s_xb = sem("s_xb")
        s_gen = sem("s_gen")
        s_blk = sem("s_blk")
        s_ev = sem("s_ev")
        s_car = sem("s_car")
        s_vio = sem("s_vio")
        s_bad = sem("s_bad")
        s_flag = sem("s_flag")
        s_sgen = sem("s_sgen")
        s_sfree = sem("s_sfree")
        s_swin = sem("s_swin")
        s_sc = sem("s_sc")
        s_sk = sem("s_sk")
        s_sdeg = sem("s_sdeg")
        s_sve = sem("s_sve")
        s_ssq = sem("s_ssq")
        s_deg = sem("s_deg")
        s_h3 = sem("s_h3")
        s_ag = sem("s_ag")
        s_age = sem("s_age")
        s_z = sem("s_z")
        s_o = sem("s_o")
        s_x1 = sem("s_x1")
        s_st = sem("s_st")
        s_lg = sem("s_lg")
        s_oho = sem("s_oho")
        s_rk = sem("s_rk")
        s_pos = sem("s_pos")
        s_te = sem("s_te")
        s_scat = sem("s_scat")
        s_xs = [sem(f"s_xs{j}") for j in range(SLOTS)]
        s_f0 = sem("s_f0")
        s_ft = sem("s_ft")
        s_fx = sem("s_fx")
        s_fh = sem("s_fh")
        s_fw = sem("s_fw")
        s_fr = sem("s_fr")
        s_fy = sem("s_fy")
        s_f2 = sem("s_f2")
        s_out = [sem(f"s_out{i}") for i in range(4)]

        block = ctx.enter_context(nc.Block())

        def chain(eng, s):
            n = [0]

            def link(ins):
                n[0] += 1
                ins.then_inc(s, 1)
                eng.wait_ge(s, n[0])
            return link

        def bad(eng, name):
            r = eng.alloc_register(name)
            eng.wait_ge(s_flag, 1)
            eng.load([r], badI[0:1, 0:1])
            return r

        def chosen(eng, name):
            regs = [eng.alloc_register(f"{name}_e{j}") for j in range(SLOTS + 1)]
            eng.wait_ge(s_te, 1)
            eng.load(regs, tei[0:1, 0:SLOTS + 1])
            return [eng.snap(r, min_val=0, max_val=NE - 1) for r in regs[:SLOTS]], regs[SLOTS]

        def holds(eng, empty, j):
            return nullcontext() if j < NT else eng.If_lt(empty, SLOTS - j)

        held = {}

        def places(eng, name, n, table, i, most):
            for r in held.get(name, []):
                eng.free_register(r)
            regs = held[name] = [eng.alloc_register(f"{name}{i + k}") for k in range(n)]
            eng.load(regs, table[0:1, i:i + n])
            return [eng.snap(r, donate=True, min_val=0, max_val=most) for r in regs]

        def spans(g):
            return sum(sum(SPANS[:s + 1]) <= GC * g for s in range(NS))

        @block.sync
        def _(eng):
            eng.dma_start(eI.rearrange("p a c two -> p (a c two)").bitcast(I32), edges.rearrange("p a c -> p (a c)")).then_inc(s_edge, 16)
            eng.dma_start(ends3, ends.rearrange("(o a) c -> o a c", o=1)).then_inc(s_place, 16)
            eng.dma_start(bnd, ends[0:1, :].broadcast_to([P, NC])).then_inc(s_edge, 16)
            eng.dma_start(begin, bases.rearrange("(a s) -> a s", a=1)).then_inc(s_sp, 16)
            eng.dma_start(dI, order).then_inc(s_end, 16)
            eng.dma_start(w0[:, :, 0:GH], gW1.rearrange("(k p) f -> p k f", p=P)).then_inc(s_gw, 16)
            eng.dma_start(b2g[:, :], gb2.rearrange("(a d) -> a d", a=1).broadcast_to([P, D])).then_inc(s_gw, 16)
            eng.dma_start(b1g[:, :], gb1.rearrange("(a d) -> a d", a=1).broadcast_to([P, GH])).then_inc(s_gw, 16)
            for i in range(3):
                eng.dma_start(w2g[i * GH:(i + 1) * GH, :], gW2).then_inc(s_gw, 16)
            eng.dma_start(w0[:, :, GH:WC], Wr.rearrange("(k p) e -> p k e", p=P)).then_inc(s_gw, 16)
            eng.dma_start(w2g[G48:G48 + 1, :], gb2.rearrange("(a d) -> a d", a=1)).then_inc(s_gw, 16)
            eng.dma_start(brb[:, :], br.rearrange("(a e) -> a e", a=1).broadcast_to([P, NE])).then_inc(s_gw, 16)
            for i in range(4):
                eng.wait_ge(s_x[i], 16)
            for e in range(NE):
                eng.dma_start(w1[:, e, :, :], fW1[e].rearrange("(k p) h -> p k h", p=P)).then_inc(s_w1, 16)
            for e in range(NE):
                eng.dma_start(w2[:, e, :, :], fW2[e].rearrange("(k p) o -> p k o", p=P)).then_inc(s_w2, 16)
            eng.dma_start(b1t[:, :, :], fb1).then_inc(s_w2, 16)
            eng.dma_start(b2f[:, :, :], fb2.rearrange("(a e) o -> a e o", a=1).broadcast_to([P, NE, D])).then_inc(s_w2, 16)
            eng.wait_ge(s_it, 1)
            for j in range(SLOTS):
                eng.dma_start(routed[j * P:(j + 1) * P, :], initr[:, :]).then_inc(s_init, 16)
            eng.wait_ge(s_scat, 16 * NT)
            empty = chosen(eng, "sp")[1]
            for j in range(SLOTS):
                with holds(eng, empty, j):
                    eng.dma_start(xs(j), routed[j * P:(j + 1) * P, :]).then_inc(s_xs[j], 16)
            for j in range(SLOTS):
                with holds(eng, empty, j):
                    eng.wait_ge(s_out[j % 4], 16 * (j // 4 + 1))

        @block.gpsimd
        def _(eng):
            eng.memset(zerob[:, :], 0.0).then_inc(s_zero, 1)
            eng.memset(identf[:, :], 0.0).then_inc(s_pl, 1)
            eng.memset(onesf[:, :], 1.0).then_inc(s_pl, 1)
            eng.iota(ir2[:, :, :], [[1, P], [0, 2]], base=0, channel_multiplier=0).then_inc(s_cst, 1)
            for w in im2:
                eng.iota(im2[w][:, :, :], [[WD, NT], [1, w], [0, 2]], base=0, channel_multiplier=0).then_inc(s_cst, 1)
            eng.wait_ge(s_pl, 2)
            eng.affine_select(out=identf[:, :], in_=identf[:, :], compare_op=ALU.not_equal, fill=1.0,
                              base=0, pattern=[[-1, P]], channel_multiplier=1).then_inc(s_cst, 1)
            for g in (0, NG // 2, 3 * NG // 4):
                eng.memset(lim[:, GC * g:GC * (g + WIDTH.count(WIDTH[g]))], 1.0 - WIDTH[g]).then_inc(s_pl2, 1)
            eng.memset(odd[:, :], 0.0).then_inc(s_pl2, 1)
            eng.memset(ct[0][:, 9:NT, :].rearrange("p q d -> p (q d)").bitcast(F32), 0.0).then_inc(s_zc, 1)
            eng.memset(initr[:, 0:D + 2], 0.0).then_inc(s_pl, 1)
            eng.memset(initr[:, D + 2:ROW].bitcast(I32), NOBODY).then_inc(s_it, 1)
            eng.memset(xt[:, :, D + 3:ROW], 0.0).then_inc(s_pl, 1)
            eng.memset(identb[:, :], 0.0).then_inc(s_pl, 1)
            eng.memset(onesb[:, :], 1.0).then_inc(s_pl, 1)
            eng.memset(upper[:, :], 1.0).then_inc(s_pl, 1)
            eng.memset(valid[:, :], 1.0).then_inc(s_pl, 1)
            eng.wait_ge(s_pl, 8)
            eng.affine_select(out=identb[:, :], in_=identb[:, :], compare_op=ALU.not_equal, fill=1.0,
                              base=0, pattern=[[-1, P]], channel_multiplier=1).then_inc(s_cst, 1)
            eng.affine_select(out=upper[:, :], in_=upper[:, :], compare_op=ALU.is_gt, fill=0.0,
                              base=0, pattern=[[1, P]], channel_multiplier=-1).then_inc(s_cst, 1)
            eng.iota(iotae[:, :, :], [[0, NT], [1, NE]], base=0, channel_multiplier=0,
                     allow_small_or_imprecise_dtypes=True).then_inc(s_cst, 1)
            eng.iota(k128[:, :, :], [[0, NE], [P, NT]], base=0, channel_multiplier=0,
                     allow_small_or_imprecise_dtypes=True).then_inc(s_cst, 1)
            eng.iota(iotaj[:, :, :], [[1, SLOTS], [0, NE]], base=0, channel_multiplier=0,
                     allow_small_or_imprecise_dtypes=True).then_inc(s_cst, 1)
            eng.iota(xt[:, :, D + 2].bitcast(I32), [[P, NT]], base=0, channel_multiplier=1).then_inc(s_cst, 1)
            eng.affine_select(out=valid[:, :], in_=valid[:, :], compare_op=ALU.is_gt, fill=0.0,
                              base=N, pattern=[[-P, NT]], channel_multiplier=-1).then_inc(s_cst, 1)
            eng.wait_ge(s_end, 16)
            eng.wait_ge(s_base, 2)
            eng.wait_ge(s_place, 16)
            eng.tensor_copy(ends3f, ends3).then_inc(s_pl2, 1)
            eng.tensor_copy(inrow, dI).then_inc(s_pl2, 1)
            eng.tensor_scalar(off, off, float(WD - SW), 0.0, ALU.add, ALU.max).then_inc(s_pl2, 1)
            eng.wait_ge(s_pl2, 7)
            eng.tensor_tensor(spn, ends3f[:, 1], ends3f[:, 0], ALU.subtract).then_inc(s_pl2, 1)
            eng.tensor_tensor(unord, inrow[:, 0:500], inrow[:, 1:501], ALU.subtract).then_inc(s_pl2, 1)
            eng.wait_ge(s_pl2, 9)
            eng.tensor_tensor(spn, spn, lim, ALU.add).then_inc(s_pl2, 1)
            eng.tensor_scalar(unord, unord, 0.0, None, ALU.max).then_inc(s_pl2, 1)
            eng.wait_ge(s_pl2, 10)
            eng.tensor_scalar(spn, spn, 0.0, None, ALU.max).then_inc(s_pl2, 1)
            eng.wait_ge(s_pl2, 12)
            eng.tensor_tensor(spn, spn, off, ALU.add).then_inc(s_pl2, 1)
            eng.wait_ge(s_gw, 16 * 9)
            for q in range(NT):
                eng.wait_ge(s_bn, q + 1)
                eng.wait_ge(s_xp, q + 1)
                eng.tensor_tensor(xt[:, q, 0:D], xt[:, q, 0:D], b2g[:, :], ALU.add).then_inc(s_xb, 1)
            eng.wait_ge(s_init, 16 * SLOTS)
            eng.wait_ge(s_st, 1)
            eng.wait_ge(s_pos, 1)
            for q in range(NT):
                r = N - q * P if q == NT - 1 else P
                eng.indirect_dma_start(
                    out=routed, out_offset=bass.IndirectOffsetOnAxis(ap=posi[0:r, q:q + 1], axis=0),
                    in_=xt[0:r, q, :], in_offset=None).then_inc(s_scat, 16)
            empty = chosen(eng, "pool")[1]
            for j in range(SLOTS):
                with holds(eng, empty, j):
                    eng.wait_ge(s_f2, j + 1)
                    eng.indirect_dma_start(
                        out=out, out_offset=bass.IndirectOffsetOnAxis(ap=xs(j)[:, D + 2:D + 3].bitcast(I32), axis=0),
                        in_=yb[:, j % 4, :], in_offset=None, bounds_check=N - 1, oob_is_err=False).then_inc(s_out[j % 4], 16)

        @block.scalar
        def _(eng):
            eng.wait_ge(s_zero, 1)
            eng.activation(ct[0][:, 6:9, :].rearrange("p q d -> p (q d)"), zerob[:, 0:1].to_broadcast([P, 3 * CW]), ACT.Copy).then_inc(s_zc, 1)
            eng.wait_ge(s_edge, 32)
            for i in range(3):
                eng.dma_start(xt[:, 3 * i:3 * i + 3, 0:D],
                              x[3 * i * P:(3 * i + 3) * P, :].rearrange("(q p) d -> p q d", p=P)).then_inc(s_x[i], 16)
            eng.wait_ge(s_pad, 1)
            eng.dma_start(xt[0:N - 9 * P, 9, 0:D], x[9 * P:N, :]).then_inc(s_x[3], 16)
            def transposed(n):
                eng.wait_ge(s_xp, n + 1)
                if n >= 2:
                    eng.wait_ge(s_h, n - 1)
                eng.activation(xnT[:, n % 2, :], PS[5][:, :], ACT.Copy).then_inc(s_xe, 1)

            eng.wait_ge(s_zc, 3)
            eng.wait_ge(s_ord, 4)
            for s in range(NS):
                if s % 15 == 0:
                    base = places(eng, "act_b", 15, baseI, s, N - 1)
                if s == 5:
                    eng.wait_ge(s_cs, 2)
                    eng.activation(w2t[:, :, :], PS[5][:, 0:4 * (G48 + 1)].rearrange("p (k f) -> p k f", k=4), ACT.Copy).then_inc(s_w2t, 1)
                if s == 42:
                    eng.wait_ge(s_ve, 1)
                    eng.activation(sm[:, 1, :], sm[:, 0, :], ACT.Sqrt).then_inc(s_sq, 1)
                for n in range(NT):
                    if sum(SPANS[:s]) <= 2 * (XB + 8 * n + 5) < sum(SPANS[:s + 1]):
                        transposed(n)
                eng.wait_ge(s_blk, s + 1)
                eng.wait_ge(s_ev, s)
                eng.activation(ct[0][:, :, bass.ds(base[s % 15] + 1, SW - 1)], span(s)[:, :, 1:SW],
                               ACT.Copy, accum_out=most[:, 0, s:s + 1]).then_inc(s_ev, 1)
            eng.wait_ge(s_ve, 2)
            eng.activation(sm[:, 1, :], sm[:, 0, :], ACT.Sqrt).then_inc(s_sq, 1)
            with eng.If_ne(bad(eng, "act_bad"), 0):
                eng.wait_ge(s_sve, 1)
                eng.activation(sm[:, 1, :], sm[:, 0, :], ACT.Sqrt).then_inc(s_ssq, 1)
            for i, (a, b) in enumerate(ABLK):
                eng.wait_ge(s_ag, i + 1)
                eng.activation(aggT[0:G48, a:b], pA[i][0:G48, 0:b - a], ACT.Copy).then_inc(s_age, 1)
            eng.wait_ge(s_ve, 3)
            eng.activation(sm[:, 1, :], sm[:, 0, :], ACT.Sqrt).then_inc(s_sq, 1)

            def routed_t(j):
                eng.wait_ge(s_ft, j + 1)
                if j >= 2:
                    eng.wait_ge(s_fh, j - 1)
                eng.activation(xnT[:, j % 2, :], PS[j % 2][:, :], ACT.Copy).then_inc(s_fx, 1)

            def weights(j):
                if j >= 2:
                    eng.wait_ge(s_fh, j - 1)
                eng.activation(w1c[:, j % 2, :, :], w1[:, ex[j], :, :].rearrange("p e k h -> p (e k) h"), ACT.Copy).then_inc(s_fw, 1)

            def relu(j):
                eng.wait_ge(s_fh, j + 1)
                if j >= 2:
                    eng.wait_ge(s_fy, j - 1)
                for m in range(2):
                    last = eng.activation(hT[:, j % 2, m * P:(m + 1) * P], PS[2 + j % 2][:, m * P:(m + 1) * P],
                                          ACT.Relu, bias=b1t[:, m, ex[j]])
                last.then_inc(s_fr, 1)

            eng.wait_ge(s_w1, 16 * NE)
            eng.wait_ge(s_w2, 16 * (NE + 2))
            ex, empty = chosen(eng, "act")
            ex = [bass.ds(e, 1) for e in ex]
            weights(0)
            weights(1)
            routed_t(0)
            for j in range(SLOTS + 1):
                if j >= 1:
                    with holds(eng, empty, j - 1):
                        relu(j - 1)
                if j + 1 < SLOTS:
                    with holds(eng, empty, j + 1):
                        if j >= 1:
                            weights(j + 1)
                        routed_t(j + 1)

        @block.tensor
        def _(eng):
            between = {}

            def weights(k):
                if k == 0:
                    eng.wait_ge(s_gw, 16 * 9)
                last = eng.matmul(pCs, onesf[:, :], w0[:, k, :], start=k == 0, stop=k == 3)
                if k == 3:
                    last.then_inc(s_cs, 1)

            def across(k):
                n = G48 + 1
                if k == 0:
                    eng.wait_ge(s_cst, 5)
                last = eng.transpose(PS[5][:, k * n:(k + 1) * n], w2g[:, k * P:(k + 1) * P], identf[0:n, 0:n])
                if k == 3:
                    last.then_inc(s_cs, 1)

            def shares(k):
                if k == 0:
                    eng.wait_ge(s_wc, 2)
                if k < 4:
                    eng.matmul(pWz, w2t[:, k, 0:G48], wc[:, k, GH:WC], start=k == 0, stop=k == 3)
                else:
                    last = eng.matmul(pBz, onesf[:, :], wb[:, k - 4, :], start=k == 4, stop=k == 7)
                    if k == 7:
                        last.then_inc(s_wz, 1)

            def turned(n, k):
                if k == 0:
                    if n % 3 == 0:
                        eng.wait_ge(s_x[n // 3], 16)
                    if n == NT - 1:
                        eng.wait_ge(s_pad, 1)
                    if n == 0:
                        eng.wait_ge(s_w2t, 1)
                    eng.wait_ge(s_xe, n)
                last = eng.transpose(PS[5][:, k * P:(k + 1) * P], xt[:, n, k * P:(k + 1) * P], identf[:, :])
                if k == 3:
                    last.then_inc(s_xp, 1)

            def times(n, k):
                if k == 0:
                    if n == 0:
                        eng.wait_ge(s_wc, 4)
                    eng.wait_ge(s_xe, n + 1)
                last = eng.matmul(pH[:, n, :], xnT[:, n % 2, k * P:(k + 1) * P], wc[:, k, :], start=k == 0, stop=k == 3)
                if k == 3:
                    last.then_inc(s_h, 1)

            for k in range(4):
                between[18 + k] = (weights, k)
                between[22 + k] = (across, k)
            for k in range(8):
                between[XB - 8 + k] = (shares, k)
            for k in range(4):
                for n in range(NT):
                    between[XB + 8 * n + k] = (turned, n, k)
                    between[XB + 8 * n + 12 + k] = (times, n, k)

            eng.wait_ge(s_zero, 1)
            eng.wait_ge(s_base, 2)
            s = at = 0
            for g in range(NG):
                if GC * g % MANY == 0:
                    offs = places(eng, "pe_o", MANY, offI, GC * g, SW - WD)
                eng.wait_ge(s_gen, g + 1)
                rows = mv[:, g % RING, 0:GC * NT * WIDTH[g]].rearrange("p (b k c) -> p b k c", b=GB, c=2)
                for i in range(GC):
                    c = GC * g + i
                    one = oh[:, g % RING, i // 2, :, i % 2]
                    if at == 0:
                        if s >= PR:
                            eng.wait_ge(s_car, s - PR + 1)
                        eng.matmul(bank(s), zerob[:, :], zeros, start=True, stop=False)
                    last = eng.matmul(span(s)[:, :, bass.ds(offs[c % MANY], WIDTH[g])], one,
                                      rows[:, i // 2, :, i % 2].rearrange("p (q i) -> p q i", q=NT),
                                      start=False, stop=at == SPANS[s] - 1)
                    at += 1
                    if at == SPANS[s]:
                        last.then_inc(s_blk, 1)
                        s, at = s + 1, 0
                    if i % 2 == 1 and c // 2 in between:
                        between[c // 2][0](*between[c // 2][1:])

            def degrees(cs):
                for k in range(NT):
                    for q in range(NT):
                        for c in cs:
                            last = eng.matmul(pDeg[:, k:k + 1], c[:, q, k * P:(k + 1) * P], onesb[:, 0:1],
                                              start=q == 0 and c is cs[0], stop=q == NT - 1 and c is cs[-1])
                return last

            eng.wait_ge(s_cst, 12)
            eng.wait_ge(s_ev, NS)
            eng.wait_ge(s_car, NS)
            degrees(ct[0:1]).then_inc(s_deg, 1)
            eng.wait_ge(s_vio, 3)
            for k in range(3):
                last = eng.matmul(pBad, odd[:, k:k + 1], onesf[:, 0:1], start=k == 0, stop=k == 2)
            last.then_inc(s_bad, 1)
            flag = bad(eng, "pe_bad")
            with eng.If_ne(flag, 0):
                ps = PS[0]
                with eng.Fori(0, NWS) as t:
                    eng.wait_ge(s_sc, eng.snap(t * 3 + 1))
                    eng.matmul(ps[:, 0:2], zerob[:, :], onesb[:, 0:2], start=True, stop=True, skip_group_check=True)
                    with eng.Fori(0, NC // 4) as b:
                        n = eng.snap(t * (NC // 4) + b)
                        eng.wait_ge(s_sgen, n + 1)
                        for i in range(4):
                            last = eng.matmul(ps[:, 0:MS], oh[:, n % 2, i // 2, :, i % 2], mvs[:, n % 2, i // 2, :, i % 2],
                                              start=False, stop=True, skip_group_check=True)
                        last.then_inc(s_sfree, 1)
                    eng.matmul(ps[:, 0:2], zerob[:, :], onesb[:, 0:2], start=False, stop=True,
                               skip_group_check=True).then_inc(s_swin, 1)
                eng.wait_ge(s_sc, 3 * NWS + 1)
                degrees(ct).then_inc(s_sdeg, 1)

            def nodes(cs):
                for k in range(NT):
                    for q in range(NT):
                        for c in cs:
                            eng.matmul(pZ[:, k, :], c[:, q, k * P:(k + 1) * P], h3[:, q, :], start=q == 0 and c is cs[0], stop=False)
                    last = eng.matmul(pZ[:, k, :], identb[:, :], h3[:, k, :], start=False, stop=True)
                last.then_inc(s_z, 1)

            def features(cs):
                for i, (a, b) in enumerate(ABLK):
                    o = pA[i][0:G48, 0:b - a]
                    for q in range(NT):
                        for c in cs:
                            eng.matmul(o, h3[:, q, :], c[:, q, a:b], start=q == 0 and c is cs[0], stop=False)
                    for k in range(a // P, b // P):
                        last = eng.matmul(pA[i][0:G48, k * P - a:(k + 1) * P - a], h3[:, k, :], identb[:, :],
                                          start=False, stop=k == b // P - 1)
                    last.then_inc(s_ag, 1)

            for layer, sums in enumerate((nodes, features)):
                eng.wait_ge(s_h3, layer + 1)
                with eng.If_ne(flag, 0):
                    sums(ct)
                with eng.Else():
                    sums(ct[0:1])
            for k in range(NT):
                eng.wait_ge(s_age, 1 + k // 4)
                if k >= 4:
                    eng.wait_ge(s_x1, k - 3)
                eng.matmul(pX[k % 4][:, :], aggT[0:G48, k * P:(k + 1) * P], w2g[0:G48, :], start=True, stop=True).then_inc(s_o, 1)
                if k == 3:
                    eng.wait_ge(s_age, 3)
                    for i in range(NT):
                        lg = eng.matmul(pLg[:, i, :], aggT[0:G48, i * P:(i + 1) * P], wz[:, :], start=True, stop=True)
                    lg.then_inc(s_lg, 1)

            eng.wait_ge(s_oho, 1)
            eng.matmul(PS[7][:, 0:NT * NE], upper[:, :], ohb, start=True, stop=False)
            eng.matmul(PS[7][:, 0:NT * NE], onesb[:, :], pre[:, 0, 7:17, :], start=False, stop=True)
            eng.matmul(pCn, onesb[:, :], pre[:, 0, 17, :], start=True, stop=True).then_inc(s_rk, 1)

            def feed(j):
                eng.wait_ge(s_f0, j + 1)
                if j >= 2:
                    eng.wait_ge(s_fx, j - 1)
                for k in range(4):
                    last = eng.transpose(PS[j % 2][:, k * P:(k + 1) * P], xn[:, j % 2, k * P:(k + 1) * P], identf[:, :])
                last.then_inc(s_ft, 1)

            def up(j):
                eng.wait_ge(s_fx, j + 1)
                eng.wait_ge(s_fw, j + 1)
                if j >= 2:
                    eng.wait_ge(s_fr, j - 1)
                for m in range(2):
                    for k in range(4):
                        last = eng.matmul(PS[2 + j % 2][:, m * P:(m + 1) * P], w1c[:, j % 2, k, m * P:(m + 1) * P],
                                          xnT[:, j % 2, k * P:(k + 1) * P], start=k == 0, stop=k == 3)
                last.then_inc(s_fh, 1)

            def down(j):
                eng.wait_ge(s_fr, j + 1)
                if j >= 2:
                    eng.wait_ge(s_f2, j - 1)
                for k in range(2):
                    last = eng.matmul(PS[6 + j % 2][:, :], hT[:, j % 2, k * P:(k + 1) * P], w2[:, ex[j], k, :],
                                      start=k == 0, stop=k == 1)
                last.then_inc(s_fy, 1)

            eng.wait_ge(s_w1, 16 * NE)
            eng.wait_ge(s_w2, 16 * (NE + 2))
            ex, empty = chosen(eng, "pe")
            feed(0)
            for j in range(SLOTS + 1):
                if j < SLOTS:
                    with holds(eng, empty, j):
                        up(j)
                if j + 1 < SLOTS:
                    with holds(eng, empty, j + 1):
                        feed(j + 1)
                if j >= 1:
                    with holds(eng, empty, j - 1):
                        down(j - 1)

        @block.vector
        def _(eng):
            link = chain(eng, s_dv)

            eng.memset(xt[96:P, NT - 1, 0:D], 0.0).then_inc(s_pad, 1)
            eng.memset(ct[0][:, 0:6, :].rearrange("p q d -> p (q d)").bitcast(F32), 0.0).then_inc(s_zc, 1)
            eng.wait_ge(s_edge, 32)
            sI, tI = eI[:, 0, :, 0], eI[:, 1, :, 0]
            eng.tensor_scalar(Q16[:, :], sI, 7, None, ALU.logical_shift_right).then_inc(s_key, 1)
            eng.tensor_scalar(R16[:, :], sI, P - 1, None, ALU.bitwise_and).then_inc(s_key, 1)
            eng.wait_ge(s_key, 1)
            eng.scalar_tensor_tensor(out=G16[:, :], in0=Q16[:, :], scalar=float(WD), in1=tI,
                                     op0=ALU.mult, op1=ALU.add).then_inc(s_key, 1)
            eng.wait_ge(s_key, 3)
            eng.tensor_tensor(G16[:, :], G16[:, :], bnd[0:KE, :], ALU.subtract).then_inc(s_key, 1)
            eng.wait_ge(s_place, 16)
            eng.tensor_tensor(off, ends3[:, 0], ends3[:, 2], ALU.subtract).then_inc(s_base, 1)
            eng.wait_ge(s_cst, 4)
            eng.wait_ge(s_key, 4)
            eng.wait_ge(s_base, 1)
            eng.tensor_scalar(offI, off, 0.0, float(SW - WD), ALU.max, ALU.min).then_inc(s_base, 1)

            def newton(r, n, link):
                v, s, a = sm[:, 0, 0:n], sm[:, 1, 0:n], sm[:, 2, 0:n]
                y = sm[:, 3, 0:n]
                link(eng.reciprocal(y, s))
                link(eng.tensor_tensor(a, y, y, ALU.mult))
                link(eng.tensor_tensor(a, a, v, ALU.mult))
                link(eng.tensor_scalar(a, a, -0.5, 1.5, ALU.mult, ALU.add))
                link(eng.tensor_tensor(r, y, a, ALU.mult))

            v, s, a, y, r = (sm[:, i, :] for i in (0, 1, 2, 3, 4))
            first = [lambda: eng.reciprocal(y, s),
                     lambda: eng.tensor_tensor(a, y, y, ALU.mult),
                     lambda: eng.tensor_tensor(a, a, v, ALU.mult),
                     lambda: eng.tensor_scalar(a, a, -0.5, 1.5, ALU.mult, ALU.add),
                     lambda: eng.tensor_tensor(r, y, a, ALU.mult)]
            base = [None]

            def carry(s):
                if s == 0:
                    eng.wait_ge(s_ord, 4)
                if s % 15 == 0:
                    base[0] = places(eng, "dve_b", 15, baseI, s, N - 1)
                eng.wait_ge(s_ev, s + 1)
                eng.wait_ge(s_car, s)
                col = ct[0][:, :, bass.ds(base[0][s % 15], 1)]
                eng.scalar_tensor_tensor(out=col, in0=span(s)[:, :, 0:1], scalar=1.0, in1=col, op0=ALU.mult, op1=ALU.add,
                                         accum_out=most[:, 1, s:s + 1]).then_inc(s_car, 1)

            def where(k):
                eng.wait_ge(s_sp, 16)
                eng.wait_ge(s_ord, k)
                if k == 0:
                    last = eng.tensor_tensor(back[:, 0:NS - 1], begin[:, 0:NS - 1], begin[:, 1:NS], ALU.subtract)
                elif k == 1:
                    last = eng.tensor_reduce(wl[:, 0:1], back[:, 0:NS - 1], X, ALU.max)
                elif k == 2:
                    last = eng.tensor_scalar(wl[:, 1:2], wl[:, 0:1], 0.0, None, ALU.is_le)
                else:
                    last = eng.tensor_scalar(baseI, begin, wl[:, 1:2], None, ALU.mult)
                last.then_inc(s_ord, 1)

            def onehot(g, o, w, i2, k):
                c = slice(GC * g, GC * (g + 1))
                return eng.tensor_tensor(
                    o, i2[:, :, :].unsqueeze(1).to_broadcast([KE, GB, w, 2]),
                    k[:, c].rearrange("p (b c) -> p b c", c=2).unsqueeze(2).to_broadcast([KE, GB, w, 2]), ALU.is_equal)

            eng.wait_ge(s_pad, 1)
            done = 0
            for g in range(NG + LAG):
                if RING <= g < NG:
                    eng.wait_ge(s_blk, spans(g - RING + 1))
                if g < NG:
                    onehot(g, oh[:, g % RING], P, ir2, R16)
                if g < 2:
                    where(2 * g)
                if done < NS and sum(SPANS[:done + 1]) <= GC * (g - LAG) + GC // 2:
                    carry(done)
                    done += 1
                if g < NG:
                    n = NT * WIDTH[g]
                    onehot(g, mv[:, g % RING, 0:GC * n].rearrange("p (b k c) -> p b k c", b=GB, c=2), n,
                           im2[WIDTH[g]], G16).then_inc(s_gen, 1)
                if g < 2:
                    where(2 * g + 1)
                while done < NS and sum(SPANS[:done + 1]) <= GC * (g - LAG + 1):
                    carry(done)
                    done += 1
                q = g // 2 - 4
                if 0 <= q < NT and g % 2 == 0:
                    if q % 3 == 0:
                        eng.wait_ge(s_x[q // 3], 16)
                    eng.bn_stats(st[:, q, :], xt[:, q, 0:D]).then_inc(s_bn, 1)
                if 0 <= q < NT and g % 2 == 1:
                    eng.wait_ge(s_bn, q + 1)
                    eng.bn_aggr(ag[:, q, :], st[:, q, :]).then_inc(s_ba, 1)
                if g == 29:
                    eng.wait_ge(s_ba, NT)
                    eng.tensor_scalar(sm[:, 0, :], ag[:, :, 1], EPS, None, ALU.add).then_inc(s_ve, 1)
                k = g - 33
                if 0 <= k < len(first):
                    eng.wait_ge(s_sq, 1)
                    eng.wait_ge(s_nw, k)
                    first[k]().then_inc(s_nw, 1)
                if g == 10:
                    eng.wait_ge(s_cs, 1)
                    eng.scalar_tensor_tensor(out=wc[:, :, :], in0=pCs.unsqueeze(1).to_broadcast([P, 4, WC]), scalar=-1.0 / D,
                                             in1=w0[:, :, :], op0=ALU.mult, op1=ALU.add).then_inc(s_wc, 1)
                if g == 11:
                    eng.wait_ge(s_wc, 1)
                    eng.wait_ge(s_w2t, 1)
                    eng.tensor_tensor(wb[:, :, :], wc[:, :, GH:WC], w2t[:, :, G48:G48 + 1].to_broadcast([P, 4, NE]), ALU.mult).then_inc(s_wc, 1)
                if g == 16:
                    eng.wait_ge(s_wz, 1)
                    eng.tensor_copy(wz[:, :], pWz).then_inc(s_wc, 1)
                    eng.tensor_copy(bz[:, :], pBz).then_inc(s_wc, 1)
                if g == 38:
                    eng.wait_ge(s_h, NT)
                    eng.wait_ge(s_wc, 4)
                    eng.tensor_tensor(xr[:, :, :], pH[:, :, GH:WC], bz[:, :].unsqueeze(1).to_broadcast([P, NT, NE]), ALU.add).then_inc(s_xr, 1)

            eng.wait_ge(s_pl2, 13)
            eng.tensor_reduce(odd[0:SROWS, 1:2], unord, X, ALU.max).then_inc(s_vio, 1)
            eng.tensor_reduce(odd[0:1, 2:3], spn, X, ALU.max).then_inc(s_vio, 1)
            eng.wait_ge(s_car, NS)
            link(eng.tensor_reduce(vio[:, :], most.rearrange("p a s -> p (a s)"), X, ALU.max))
            eng.tensor_scalar(odd[:, 0:1], vio[:, :], 256.0, None, ALU.is_gt).then_inc(s_vio, 1)
            eng.wait_ge(s_deg, 1)
            eng.tensor_scalar(sm[:, 0, :], pDeg, 1.0, None, ALU.add).then_inc(s_ve, 1)
            eng.wait_ge(s_bad, 1)
            eng.tensor_copy(badI[:, 0:1], pBad).then_inc(s_flag, 1)
            flag = bad(eng, "dve_bad")
            eng.wait_ge(s_sq, 2)
            dinv = sm[:, 5, :]
            newton(dinv, NT, link)
            with eng.If_ne(flag, 0):
                slink = chain(eng, s_sk)
                slink(eng.scalar_tensor_tensor(out=K16, in0=tI, scalar=float(NT), in1=Q16[:, :],
                                               op0=ALU.mult, op1=ALU.add))
                for a in range(0, MS, MC):
                    n = min(MC, MS - a)
                    last = eng.tensor_scalar(tw[:, a:a + n, :], im2[WD][:, 0:n, :], float(a), None, ALU.add)
                slink(last)
                eng.sem_inc(s_sfree, 2)
                eng.sem_inc(s_sc, 1)
                with eng.Fori(0, NWS) as t:
                    with eng.Fori(0, NC // 4) as b:
                        n = eng.snap(t * (NC // 4) + b)
                        eng.wait_ge(s_sfree, n + 1)
                        for o, w, i2, k in ((oh[:, n % 2, 0:2], P, ir2, R16), (mvs[:, n % 2], MS, tw, K16)):
                            last = eng.tensor_tensor(
                                o, i2[:, :, :].unsqueeze(1).to_broadcast([KE, 2, w, 2]),
                                k[:, bass.ds(b * 4, 4)].rearrange("p (b c) -> p b c", c=2).unsqueeze(2).to_broadcast([KE, 2, w, 2]),
                                ALU.is_equal)
                        last.then_inc(s_sgen, 1)
                    eng.wait_ge(s_sgen, eng.snap(t * (NC // 4) + NC // 4))
                    eng.tensor_scalar(tw[:, :, :], tw[:, :, :], float(MS), None, ALU.add).then_inc(s_sc, 1)
                    eng.wait_ge(s_swin, t + 1)
                    p = PS[0][:, 0:MS].rearrange("p (i q) -> p q i", q=NT)
                    to = bass.ds(t * WS, WS)
                    eng.tensor_copy(ct[0][:, :, to], p).then_inc(s_sc, 1)
                    eng.wait_ge(s_sc, eng.snap(t * 3 + 3))
                    eng.tensor_tensor(ct[1][:, :, to], p, ct[0][:, :, to], ALU.subtract).then_inc(s_sc, 1)
                eng.wait_ge(s_sdeg, 1)
                eng.tensor_scalar(sm[:, 0, :], pDeg, 1.0, None, ALU.add).then_inc(s_sve, 1)
                eng.wait_ge(s_ssq, 1)
                newton(dinv, NT, slink)
            db = dinv.unsqueeze(2).to_broadcast([P, NT, GH])

            def split(a):
                link(eng.tensor_copy(h3[:, :, 0:GH], a))
                link(eng.tensor_tensor(gsm[:, 1], a, h3[:, :, 0:GH], ALU.subtract))
                link(eng.tensor_copy(h3[:, :, GH:2 * GH], gsm[:, 1]))
                eng.tensor_tensor(h3[:, :, 2 * GH:G48], gsm[:, 1], h3[:, :, GH:2 * GH], ALU.subtract).then_inc(s_h3, 1)

            link(eng.tensor_tensor(sm[:, 3, :], dinv, sm[:, 4, :], ALU.mult))
            link(eng.tensor_tensor(gsm[:, 0], pH[:, :, 0:GH], sm[:, 3, :].unsqueeze(2).to_broadcast([P, NT, GH]), ALU.mult))
            split(gsm[:, 0])
            eng.wait_ge(s_z, 1)
            link(eng.tensor_reduce(gsm[:, 1], pZ.rearrange("p q (a f) -> p q f a", a=3), X, ALU.add))
            link(eng.tensor_tensor(gsm[:, 2], gsm[:, 1], db, ALU.mult))
            link(eng.tensor_tensor(gsm[:, 3], gsm[:, 2], b1g[:, :].unsqueeze(1).to_broadcast([P, NT, GH]), ALU.add))
            link(eng.scalar_tensor_tensor(out=gsm[:, 0], in0=gsm[:, 3], scalar=0.0, in1=db, op0=ALU.max, op1=ALU.mult))
            split(gsm[:, 0])

            eng.wait_ge(s_xb, NT)
            for q in range(NT + 2):
                if q < NT:
                    eng.wait_ge(s_o, q + 1)
                    eng.scalar_tensor_tensor(out=xt[:, q, 0:D], in0=pX[q % 4][:, :], scalar=dinv[:, q:q + 1],
                                             in1=xt[:, q, 0:D], op0=ALU.mult, op1=ALU.add).then_inc(s_x1, 1)
                if 1 <= q <= NT:
                    eng.wait_ge(s_x1, q)
                    eng.bn_stats(st[:, q - 1, :], xt[:, q - 1, 0:D]).then_inc(s_bn, 1)
                if q >= 2:
                    eng.wait_ge(s_bn, NT + q - 1)
                    eng.bn_aggr(ag[:, q - 2, :], st[:, q - 2, :]).then_inc(s_ba, 1)
            eng.wait_ge(s_ba, 2 * NT)
            eng.tensor_scalar(sm[:, 0, :], ag[:, :, 1], EPS, None, ALU.add).then_inc(s_ve, 1)
            eng.wait_ge(s_lg, 1)
            eng.wait_ge(s_xr, 1)
            link(eng.tensor_tensor(rt[:, 4], pLg, dinv.unsqueeze(2).to_broadcast([P, NT, NE]), ALU.mult))
            link(eng.tensor_tensor(rt[:, 5], rt[:, 4], xr[:, :, :], ALU.add))
            for i in range(2):
                eng.memset(pre[:, i, 0:8, :], 0.0)
                link(eng.memset(epre[:, i, 0:4], 0.0))
            eng.wait_ge(s_sq, 3)
            rstd = xt[:, :, D]
            newton(rstd, NT, link)
            eng.scalar_tensor_tensor(out=xt[:, :, D + 1], in0=ag[:, :, 0], scalar=-1.0, in1=rstd,
                                     op0=ALU.mult, op1=ALU.mult).then_inc(s_st, 1)
            link(eng.tensor_tensor(rt[:, 4], rt[:, 5], rstd.unsqueeze(2).to_broadcast([P, NT, NE]), ALU.mult))

            link(eng.tensor_tensor(rt[:, 0], rt[:, 4], brb[:, :].unsqueeze(1).to_broadcast([P, NT, NE]), ALU.add))
            link(eng.tensor_reduce(sm[:, 2, :], rt[:, 0], X, ALU.max))
            link(eng.tensor_tensor(rt[:, 1], rt[:, 0], sm[:, 2, :].unsqueeze(2).to_broadcast([P, NT, NE]), ALU.is_equal))
            link(eng.scalar_tensor_tensor(out=rt[:, 2], in0=rt[:, 1], scalar=-float(NE), in1=iotae[:, :, :],
                                          op0=ALU.mult, op1=ALU.add))
            link(eng.tensor_reduce(sm[:, 3, :], rt[:, 2], X, ALU.min))
            link(eng.tensor_tensor(rt[:, 1], rt[:, 2], sm[:, 3, :].unsqueeze(2).to_broadcast([P, NT, NE]), ALU.is_equal))
            link(eng.tensor_tensor(rt[:, 3], rt[:, 1], valid[:, :].unsqueeze(2).to_broadcast([P, NT, NE]), ALU.mult))
            link(eng.tensor_copy(ohb, rt[:, 3]))
            link(eng.tensor_copy(pre[:, 0, 8:18, :], rt[:, 3]))
            for i, s in enumerate((1, 2, 4, 8)):
                ins = eng.tensor_tensor(pre[:, 1 - i % 2, 8:18, :], pre[:, i % 2, 8:18, :], pre[:, i % 2, 8 - s:18 - s, :], ALU.add)
                if s < 8:
                    link(ins)
                else:
                    ins.then_inc(s_oho, 1)
            eng.wait_ge(s_rk, 1)
            link(eng.tensor_tensor(cmp_, pCn.unsqueeze(2).to_broadcast([P, NE, NT]), k128[:, :, :], ALU.is_gt))
            link(eng.tensor_reduce(epre[:, 0, 4:12], cmp_, X, ALU.add))
            for i, s in enumerate((1, 2, 4)):
                link(eng.tensor_tensor(epre[:, 1 - i % 2, 4:12], epre[:, i % 2, 4:12], epre[:, i % 2, 4 - s:12 - s], ALU.add))
            link(eng.scalar_tensor_tensor(out=rt[:, 4], in0=epre[:, 1, 3:11].unsqueeze(1).to_broadcast([P, NT, NE]),
                                          scalar=float(P), in1=pRk, op0=ALU.mult, op1=ALU.add))
            link(eng.tensor_tensor(rt[:, 5], rt[:, 4], rt[:, 3], ALU.mult))
            link(eng.tensor_reduce(sm[:, 2, :], rt[:, 5], X, ALU.add))
            eng.tensor_copy(posi[:, :], sm[:, 2, :]).then_inc(s_pos, 1)
            link(eng.tensor_tensor(cmj[0:1], epre[0:1, 1, 4:12].unsqueeze(1).to_broadcast([1, SLOTS, NE]),
                                   iotaj[:, :, :], ALU.is_le))
            link(eng.tensor_reduce(tef[0:1, 0:SLOTS], cmj[0:1], X, ALU.add))
            link(eng.tensor_scalar(tef[0:1, 0:SLOTS], tef[0:1, 0:SLOTS], float(NE - 1), None, ALU.min))
            link(eng.tensor_scalar(tef[0:1, SLOTS:SLOTS + 1], epre[0:1, 1, 11:12], -1.0, float(SLOTS), ALU.mult, ALU.add))
            eng.tensor_copy(tei[:, 0:SLOTS + 1], tef[0:1, 0:SLOTS + 1]).then_inc(s_te, 1)
            ex, empty = chosen(eng, "dve")

            def ready(j):
                eng.wait_ge(s_xs[j], 16)
                if j >= 2:
                    eng.wait_ge(s_ft, j - 1)
                eng.tensor_scalar(xn[:, j % 2, :], xs(j)[:, 0:D], xs(j)[:, D:D + 1], xs(j)[:, D + 1:D + 2],
                                  ALU.mult, ALU.add).then_inc(s_f0, 1)

            def final(j):
                eng.wait_ge(s_fy, j + 1)
                if j >= 4:
                    eng.wait_ge(s_out[j % 4], 16 * (j // 4))
                y = yb[:, j % 4, :]
                link(eng.tensor_tensor(y, PS[6 + j % 2][:, :], b2f[:, ex[j], :], ALU.add))
                eng.tensor_tensor(y, y, xs(j)[:, 0:D], ALU.add).then_inc(s_f2, 1)

            eng.wait_ge(s_w2, 16 * (NE + 2))
            ready(0)
            ready(1)
            for j in range(SLOTS + 1):
                if j + 2 < SLOTS:
                    with holds(eng, empty, j + 2):
                        ready(j + 2)
                if j >= 1:
                    with holds(eng, empty, j - 1):
                        final(j - 1)


_INS = ["x", "src", "dst", "ends", "bases", "L0_gnn_W1", "L0_gnn_b1", "L0_gnn_W2", "L0_gnn_b2", "L0_ffn_Wr", "L0_ffn_br",
        "L0_ffn_W1", "L0_ffn_b1", "L0_ffn_W2", "L0_ffn_b2"]


def kernel(**inputs):
    import numpy as _np
    import concourse.bacc as _bacc
    from concourse import mybir as _mybir
    from concourse.bass_utils import run_bass_kernel_spmd as _run

    nc = _bacc.Bacc("TRN2", target_bir_lowering=False, num_devices=1)
    arrays, args = {}, []
    for name in _INS:
        a = _np.ascontiguousarray(inputs["dst" if name in ("ends", "bases") else name])
        if name == "src":
            e = _np.stack([a, _np.asarray(inputs["dst"])]).reshape(2, NC, KE)
            a = _np.ascontiguousarray(e.transpose(2, 0, 1))
        elif name == "dst":
            n = len(a) // SROWS
            a = _np.stack([_np.append(a, a[-1])[n * r:n * r + n + 1] for r in range(SROWS)])
        elif name == "bases":
            a = _np.ascontiguousarray(a[0::KE][_np.cumsum([0] + SPANS[:-1])])
        elif name == "ends":
            a, z = a[0::KE], a[KE - 1::KE]
            a = _np.stack([a, z, _np.repeat(a[_np.cumsum([0] + SPANS[:-1])], SPANS)])
        elif name == "L0_ffn_b1":
            a = _np.ascontiguousarray(a.reshape(NE, 2, P).transpose(2, 1, 0))
        arrays[f"in_{name}"] = a
        args.append(nc.dram_tensor(f"in_{name}", a.shape, _mybir.dt.from_np(a.dtype), kind="ExternalInput").ap())
    args.append(nc.dram_tensor("out_0", (N, D), F32, kind="ExternalOutput").ap())
    program(nc, *args)
    r = _run(nc, [arrays], core_ids=[0])
    return r.results[0]["out_0"]
```
